# Optimizing a Trainium2 kernel written in Bass

```python
import numpy as np
import jax
import jax.numpy as jnp

def _softmax(x, axis=-1):
    return jax.nn.softmax(x, axis=axis)

def _gelu(x):
    return jax.nn.gelu(x, approximate=True)

def _silu(x):
    return jax.nn.silu(x)

def _sigmoid(x):
    return jax.nn.sigmoid(x)

def _layernorm(x, axis=-1, eps=1e-05):
    m = jnp.mean(x, axis=axis, keepdims=True)
    v = jnp.var(x, axis=axis, keepdims=True)
    return (x - m) / jnp.sqrt(v + eps)

def _scatter_add(tgt, idx, src, axis=0):
    return tgt.at[idx].add(src)

def _segment_sum(src, seg, n):
    return jax.ops.segment_sum(src, seg, n)
kernel_name = 'mk_adj_preln_d2_adj_r2_bed755'

def setup_inputs(seed: int=0):
    np.random.seed(seed)
    _w = jnp.asarray

    def _rec_inputs():
        import jax
        import jax.numpy as jnp
        _gk = jax.random.key(seed)
        x = -0.0006008 + 1.001 * jax.random.normal(jax.random.fold_in(_gk, 1), (4096, 128), jnp.float32)
        _w = (1.0 + jnp.arange(4096, dtype=jnp.float32)) ** (-0.5)
        _w = _w / _w.mean()
        _pij = jnp.clip(0.00195312 * _w[:, None] * _w[None, :], 0.0, 1.0)
        _a = jax.random.uniform(jax.random.fold_in(_gk, 2), (4096, 4096)) < _pij
        _a = jnp.logical_or(_a, jnp.eye(4096, dtype=bool))
        _af = _a.astype(jnp.float32)
        _af = _af * jax.random.uniform(jax.random.fold_in(_gk, 3), (4096, 4096), jnp.float32, 0.05, 1)
        adj = _af
        return (x, adj)
    x, adj = _rec_inputs()

    def _L0_gnn_setup():
        import jax, jax.numpy as jnp
        import numpy as np
        N = 5000
        F = 128
        key = jax.random.key(seed)
        k1, k2 = jax.random.split(key)
        x = jax.random.normal(k1, (N, F), dtype=jnp.float32)
        A = jax.random.uniform(k2, (N, N), dtype=jnp.float32)
        W = jnp.ones((F,), dtype=jnp.float32)
        return {'input': x, 'A': A, 'W': W}
    _L0_gnn_all = _L0_gnn_setup()
    _L0_gnn_in = {k: v for k, v in _L0_gnn_all.items() if k in ('W',)}
    del _L0_gnn_all

    def _L1_gnn_setup():
        import jax, jax.numpy as jnp
        import numpy as np
        N = 4096
        C = 128
        key = jax.random.key(seed)
        k1, k2, k3 = jax.random.split(key, 3)
        x = jax.random.normal(k1, (N, C), dtype=jnp.float32)
        evals = jax.random.uniform(k2, (N,), dtype=jnp.float32)
        evecs = jax.random.normal(k3, (N, N), dtype=jnp.float32)
        t = jnp.ones((1,), dtype=jnp.float32)
        return {'x': x, 'evals': evals, 'evecs': evecs, 't': t}
    _L1_gnn_all = _L1_gnn_setup()
    _L1_gnn_in = {k: v for k, v in _L1_gnn_all.items() if k in ('evals', 't')}
    del _L1_gnn_all
    return {'x': x, 'adj': adj, 'L0_gnn_W': _L0_gnn_in['W'], 'L1_gnn_evals': _L1_gnn_in['evals'], 'L1_gnn_t': _L1_gnn_in['t']}

def reference(x, adj, L0_gnn_W, L1_gnn_evals, L1_gnn_t):
    import jax
    import jax.numpy as jnp

    def _L0_gnn_ref(input, A, W):
        import jax, jax.numpy as jnp
        import numpy as np
        N = 5000
        F = 128
        hidden = input * W
        return A @ hidden

    def _L1_gnn_ref(x, evals, evecs, t):
        import jax, jax.numpy as jnp
        import numpy as np
        N = 4096
        C = 128
        t_eff = jnp.clip(t[0], 1e-08, None)
        x_spec = jnp.einsum('nk,nc->kc', evecs, x)
        coefs = jnp.exp(-evals * t_eff)[:, None]
        out = jnp.einsum('nk,kc->nc', evecs, coefs * x_spec)
        return out
    h = jnp.maximum(_layernorm(x, axis=-1), 0.0)
    x = x + _L0_gnn_ref(h, adj, L0_gnn_W)
    h = jnp.maximum(_layernorm(x, axis=-1), 0.0)
    x = x + _L1_gnn_ref(h, L1_gnn_evals, adj, L1_gnn_t)
    return x

_drawn_inputs = setup_inputs


def setup_inputs(seed=0):
    import zlib

    import numpy as np

    out = dict(_drawn_inputs(seed))
    spreads = {'L0_gnn_W': (1.0, 0.2)}
    factors = {}
    for name, (base, spread) in spreads.items():
        noise = np.random.default_rng([zlib.crc32(name.encode()), seed]).standard_normal(out[name].shape)
        drawn = base * np.exp(spread * noise) if base else spread * noise
        out[name] = jnp.asarray(drawn.astype(out[name].dtype))
    for name, factor in factors.items():
        out[name] = (out[name] * factor).astype(out[name].dtype)
    return out
```

```python
from contextlib import ExitStack

import concourse.bass as bass
from concourse import mybir

F32 = mybir.dt.float32
F32R = mybir.dt.float32r
ALU = mybir.AluOpType
ACT = mybir.ActivationFunctionType

P = 128
TN = 2
ROWS = TN * P
TK = 4
COLS = TK * P
EPS = 1e-5
T_MIN = 1e-8
N_AT = 4
N_NAT = 4
TURN_LAG = 2
SPEC_LAG = 14
SPLIT_LAG = 11


class Step:

    def __init__(self, j, q0=0, b0=0):
        self.j, self.q0, self.b0 = j, q0, b0

    def back(self, n):
        return Step(self.j - n, self.q0, self.b0)

    def ran(self, n):
        return not isinstance(self.q0, int) or self.j >= n

    def done(self):
        return self.q0 + (self.j + 1)

    def block(self):
        return self.b0 + self.j // 8

    def blocks(self, n=1):
        return self.b0 + (self.j // 8 + n)

    @property
    def chunk(self):
        return self.j % 8

    @property
    def parity(self):
        return self.j // 8 % 2


def program(nc, x, adj, w0, evals, t, out):
    N, C = x.shape
    NT = N // P
    BLOCKS = N // ROWS
    CHUNKS = N // COLS
    STEPS = BLOCKS * CHUNKS
    PAIR = 2 * CHUNKS
    PAIRS = STEPS // PAIR
    OVERLAP = STEPS - (STEPS + SPEC_LAG + 1 - CHUNKS)
    assert C == P and CHUNKS == 8 and BLOCKS % 2 == 0
    X_PIECES = 4
    PT = NT // X_PIECES

    with ExitStack() as ctx:
        def sb(name, shape, dt=F32):
            return ctx.enter_context(nc.sbuf_tensor(name, shape, dt))

        def psum(name, shape):
            return ctx.enter_context(nc.psum_tensor(name, shape, F32))

        def sem(name):
            return ctx.enter_context(nc.semaphore(name))

        nat = [sb(f"nat{i}", [P, TN, 2 * COLS]) for i in range(PAIR // 2)]
        at = [sb(f"at{i}", [P, 2, TK, ROWS], F32R) for i in range(N_AT)]
        nsp = [sb(f"nsp{i}", [P, 2, TN, COLS], F32R) for i in range(N_NAT)]
        wt = sb("wt", [P, 2, NT, C], F32R)
        h1 = [sb(f"h1_{i}", [P, 2, TN, C], F32R) for i in range(2)]
        xs = sb("xs", [P, NT, C])
        spec = sb("spec", [P, N])
        ident = sb("ident", [P, P])
        w_all = sb("w_all", [P, C])
        half = sb("half", [P, ROWS])
        fold = sb("fold", [P, ROWS])
        z1 = sb("z1", [P, TN, C])
        z0 = [sb(f"z0_{i}", [P, TK, C]) for i in range(2)]
        stats = sb("stats", [P, PT, 6])
        mv0 = sb("mv0", [P, NT, 2])
        mv1 = sb("mv1", [P, TN, 2])
        rstd0 = sb("rstd0", [P, NT])
        rstd1 = sb("rstd1", [P, TN])
        lnv = sb("lnv", [P, 6, PT])
        tneg = sb("tneg", [P, 1])
        coef = sb("coef", [P, NT])

        turn = [psum(f"turn{i}", [P, TK, ROWS]) for i in range(2)]
        prod = [psum(f"prod{i}", [P, 2 * ROWS]) for i in range(2)]
        part = [psum(f"part{i}", [P, COLS]) for i in range(2)]

        x_loaded = [sem(f"x_loaded{i}") for i in range(X_PIECES)]
        w_loaded, t_loaded, ev_loaded = sem("w_loaded"), sem("t_loaded"), sem("ev_loaded")
        nat_loaded = [sem(f"nat_loaded{i}") for i in range(PAIR // 2)]
        stored = sem("stored")
        zeroed, ident_ready, ev_zeroed = sem("zeroed"), sem("ident_ready"), sem("ev_zeroed")
        spec_zeroed = sem("spec_zeroed")
        t_ready, ev_turned, coef_ready = sem("t_ready"), sem("ev_turned"), sem("coef_ready")
        turned, at_hi, at_lo, projected = sem("turned"), sem("at_hi"), sem("at_lo"), sem("projected")
        nat_hi, nat_lo, spectral, summed = sem("nat_hi"), sem("nat_lo"), sem("spectral"), sem("summed")
        half_ready, fold_ready, rows_turned = sem("half_ready"), sem("fold_ready"), sem("rows_turned")
        x_ready, z1_ready = sem("x_ready"), sem("z1_ready")
        h1_hi, h1_lo = sem("h1_hi"), sem("h1_lo")
        ln_stats, ln_moments, ln_var, ln_sqrt = sem("ln_stats"), sem("ln_moments"), sem("ln_var"), sem("ln_sqrt")
        ln_recip, ln_square, ln_resid, ln_factor = sem("ln_recip"), sem("ln_square"), sem("ln_resid"), sem("ln_factor")
        ln_rstd = sem("ln_rstd")
        z0_ready, w0_ready, w0_hi, w0_lo = sem("z0_ready"), sem("w0_ready"), sem("w0_hi"), sem("w0_lo")
        sp_turned, sp_scaled, sp_hi, sp_lo = sem("sp_turned"), sem("sp_scaled"), sem("sp_hi"), sem("sp_lo")

        adj_v = adj.rearrange("(b t p) k -> b p t k", t=TN, p=P)
        out_v = out.rearrange("(b t p) c -> b p t c", t=TN, p=P)
        x_v = x.rearrange("(t p) c -> p t c", p=P)
        ev_rows = z1[:, 0, :]

        SP_TURN = STEPS + SPEC_LAG + 1 - CHUNKS
        SWEEP2 = SP_TURN
        TAIL_END = SWEEP2 + PAIR

        def second(s):
            return Step(STEPS + s - SWEEP2)

        block = ctx.enter_context(nc.Block())

        @block.sync
        def _(sp):
            def load(step, source_block):
                slot = step.j % PAIR // 2
                c = step.chunk
                sp.dma_start(nat[slot][:], adj_v[source_block, :, :, c * COLS:(c + 2) * COLS]
                             ).then_inc(nat_loaded[slot], 16)

            for j in range(0, PAIR, 2):
                load(Step(j), j // CHUNKS)
            with sp.Fori(1, PAIRS) as pair:
                q0, b0 = sp.snap(pair * PAIR), sp.snap(pair * 2)
                for j in range(0, PAIR, 2):
                    step = Step(j, q0, b0)
                    sp.wait_ge(nat_lo, step.back(PAIR - 1).done())
                    load(step, step.block())
            with sp.Fori(PAIRS + 1, 2 * PAIRS) as pair:
                q0, b0 = sp.snap(pair * PAIR), sp.snap(pair * 2)
                source = sp.snap(b0 - (BLOCKS + 2))
                for j in range(0, PAIR, 2):
                    step = Step(j, q0, b0)
                    sp.wait_ge(turned, step.back(PAIR - 1).done())
                    load(step, source + j // CHUNKS)

        @block.gpsimd
        def _(pool):
            nc.gpsimd.memset(ident[:], 0.0).then_inc(zeroed, 1)
            nc.gpsimd.memset(ev_rows, 0.0).then_inc(ev_zeroed, 1)
            pool.wait_ge(zeroed, 1)
            nc.gpsimd.affine_select(out=ident[:], in_=ident[:], compare_op=ALU.not_equal, fill=1.0, base=0,
                                    pattern=[[-1, P]], channel_multiplier=1).then_inc(ident_ready, 1)

            def norm_rows(g):
                if g % 2 == 0:
                    pool.wait_ge(ln_rstd, g * TK // PT + 1)
                if g >= 2:
                    pool.wait_ge(w0_lo, g - 1)
                for i in range(TK):
                    n = g * TK + i
                    last = nc.gpsimd.tensor_scalar(z0[g % 2][:, i, :], xs[:, n, :], mv0[:, n, 0:1],
                                                   rstd0[:, n:n + 1], ALU.subtract, ALU.mult)
                last.then_inc(z0_ready, 1)

            def low_rows(g):
                pool.wait_ge(w0_hi, g + 1)
                nc.gpsimd.tensor_tensor(wt[:, 1, g * TK:(g + 1) * TK, :], z0[g % 2][:],
                                        wt[:, 0, g * TK:(g + 1) * TK, :], ALU.subtract).then_inc(w0_lo, 1)

            def low_nat(step):
                pool.wait_ge(nat_hi, step.done())
                slot, c = step.j % PAIR // 2, step.j % 2
                nc.gpsimd.tensor_tensor(nsp[step.j % N_NAT][:, 1], nat[slot][:, :, c * COLS:(c + 1) * COLS],
                                        nsp[step.j % N_NAT][:, 0], ALU.subtract).then_inc(nat_lo, 1)

            norm_rows(0)
            for j in range(PAIR):
                if j + 1 < CHUNKS:
                    norm_rows(j + 1)
                if j < CHUNKS:
                    low_rows(j)
                if j == CHUNKS:
                    nc.gpsimd.memset(spec[:], 0.0).then_inc(spec_zeroed, 1)
                if j >= SPLIT_LAG:
                    low_nat(Step(j - SPLIT_LAG))
            with pool.Fori(1, PAIRS) as pair:
                q0 = pool.snap(pair * PAIR)
                for j in range(PAIR):
                    low_nat(Step(j, q0).back(SPLIT_LAG))
            for s in range(STEPS, STEPS + SPLIT_LAG):
                low_nat(Step(s - SPLIT_LAG))

            for b in range(2):
                pool.wait_ge(x_ready, BLOCKS + b + 1)
                row = BLOCKS - 2 + b
                pool.dma_start(out_v[row], xs[:, row * TN:(row + 1) * TN, :]).then_inc(stored, 16)
            with pool.Fori(0, BLOCKS - 2) as row:
                pool.wait_ge(x_ready, pool.snap(row + (BLOCKS + 3)))
                pool.dma_start(out_v[row], xs[:, bass.ds(row * TN, TN), :]).then_inc(stored, 16)
            pool.wait_ge(stored, 16 * BLOCKS)

        @block.scalar
        def _(act):
            act.dma_start(xs[:, 0:PT, :], x_v[:, 0:PT, :]).then_inc(x_loaded[0], 16)
            act.wait_ge(ev_zeroed, 1)
            act.dma_start(ev_rows[0:NT, :], evals.rearrange("(t p) -> t p", p=P)).then_inc(ev_loaded, 16)
            act.dma_start(tneg[:], t.rearrange("(a b) -> a b", a=1).partition_broadcast(P)
                          ).then_inc(t_loaded, 16)
            act.dma_start(w_all[:], w0.rearrange("(a b) -> a b", a=1).partition_broadcast(P)
                          ).then_inc(w_loaded, 16)
            for i in range(1, X_PIECES):
                act.dma_start(xs[:, i * PT:(i + 1) * PT, :], x_v[:, i * PT:(i + 1) * PT, :]
                              ).then_inc(x_loaded[i], 16)
            act.wait_ge(t_ready, 1)
            act.wait_ge(ev_turned, 1)
            nc.scalar.activation(coef[:], prod[1][:, 0:NT], ACT.Exp, scale=tneg[:, 0:1]).then_inc(coef_ready, 1)

            def root(n, tiles):
                act.wait_ge(ln_var, n)
                nc.scalar.activation(lnv[:, 1, 0:tiles], lnv[:, 0, 0:tiles], ACT.Sqrt).then_inc(ln_sqrt, 1)

            def high_rows(g):
                act.wait_ge(w0_ready, g + 1)
                nc.scalar.activation(wt[:, 0, g * TK:(g + 1) * TK, :], z0[g % 2][:], ACT.Copy
                                     ).then_inc(w0_hi, 1)

            def high_turned(step):
                act.wait_ge(turned, step.done())
                if step.ran(N_AT):
                    act.wait_ge(projected, step.back(N_AT).done())
                nc.scalar.activation(at[step.j % N_AT][:, 0], turn[step.j % 2][:], ACT.Copy).then_inc(at_hi, 1)

            def high_nat(step):
                if step.ran(N_NAT):
                    act.wait_ge(spectral, step.back(N_NAT).done())
                slot, c = step.j % PAIR // 2, step.j % 2
                nc.scalar.activation(nsp[step.j % N_NAT][:, 0], nat[slot][:, :, c * COLS:(c + 1) * COLS],
                                     ACT.Copy).then_inc(nat_hi, 1)

            def copy_half(last):
                act.wait_ge(projected, last.done())
                if last.ran(CHUNKS):
                    act.wait_ge(fold_ready, last.blocks(0))
                nc.scalar.activation(half[:], prod[last.parity][:, ROWS:2 * ROWS], ACT.Copy
                                     ).then_inc(half_ready, 1)

            def high_h1(last):
                act.wait_ge(z1_ready, last.blocks())
                nc.scalar.activation(h1[last.parity][:, 0], z1[:], ACT.Relu).then_inc(h1_hi, 1)

            def first_sweep(step, turning=True):
                if step.chunk == 2 and step.ran(CHUNKS):
                    copy_half(step.back(3))
                if turning:
                    high_turned(step)
                if step.chunk == 4 and step.ran(CHUNKS):
                    high_h1(step.back(5))
                if step.ran(SPLIT_LAG):
                    high_nat(step.back(SPLIT_LAG))
                if step.chunk == 3 and step.ran(CHUNKS):
                    root(step.back(4).blocks(X_PIECES + 1), TN)

            root(1, PT)
            for j in range(PAIR):
                if j < CHUNKS:
                    high_rows(j)
                first_sweep(Step(j))
                if j % 2 == 0 and j // 2 + 1 < X_PIECES:
                    root(j // 2 + 2, PT)
            with act.Fori(1, PAIRS) as pair:
                q0, b0 = act.snap(pair * PAIR), act.snap(pair * 2)
                for j in range(PAIR):
                    first_sweep(Step(j, q0, b0))

            def high_spectrum(c):
                act.wait_ge(sp_scaled, c + 1)
                nc.scalar.activation(wt[:, 0, c * TK:(c + 1) * TK, :], z0[c % 2][:], ACT.Copy).then_inc(sp_hi, 1)

            def second_sweep(step, turning=True):
                if step.chunk == 2 and (step.j >= CHUNKS):
                    copy_half(step.back(3))
                if turning:
                    high_turned(step)

            for s in range(STEPS, TAIL_END):
                if s < STEPS + SPLIT_LAG:
                    if s == STEPS + 2:
                        copy_half(Step(s).back(3))
                    if s == STEPS + 4:
                        high_h1(Step(s).back(5))
                    high_nat(Step(s - SPLIT_LAG))
                    if s == STEPS + 3:
                        root(Step(s).back(4).blocks(X_PIECES + 1), TN)
                if 0 <= s - SP_TURN - 1 < CHUNKS:
                    high_spectrum(s - SP_TURN - 1)
                if s >= SWEEP2:
                    q = second(s)
                    if q.chunk == 2 and q.j >= STEPS + CHUNKS:
                        copy_half(q.back(3))
                    high_turned(q)
            with act.Fori(PAIRS + 1, 2 * PAIRS) as pair:
                q0, b0 = act.snap(pair * PAIR), act.snap(pair * 2)
                for j in range(PAIR):
                    q = Step(j, q0, b0)
                    if q.chunk == 2:
                        copy_half(q.back(3))
                    high_turned(q)
            copy_half(Step(2 * STEPS - 1))

        @block.vector
        def _(dve):
            dve.wait_ge(t_loaded, 16)
            nc.vector.tensor_scalar(tneg[:], tneg[:], T_MIN, -1.0, ALU.max, ALU.mult).then_inc(t_ready, 1)

            def row_stats(rows, tiles):
                for i in range(tiles):
                    last = nc.vector.bn_stats(stats[:, i, :], rows[:, i, :])
                last.then_inc(ln_stats, 1)

            def moments(n, mv, tiles):
                for i in range(tiles):
                    last = nc.vector.bn_aggr(mv[:, i, :], stats[:, i, :])
                last.then_inc(ln_moments, 1)
                dve.wait_ge(ln_moments, n)
                nc.vector.tensor_scalar(lnv[:, 0, 0:tiles], mv[:, :, 1], EPS, None, ALU.add).then_inc(ln_var, 1)

            def inverse_root(n, rstd, tiles):
                v, root, r, rr, vrr, f = (lnv[:, i, 0:tiles] for i in range(6))
                dve.wait_ge(ln_sqrt, n)
                nc.vector.reciprocal(r, root).then_inc(ln_recip, 1)
                dve.wait_ge(ln_recip, n)
                nc.vector.tensor_tensor(rr, r, r, ALU.mult).then_inc(ln_square, 1)
                dve.wait_ge(ln_square, n)
                nc.vector.tensor_tensor(vrr, rr, v, ALU.mult).then_inc(ln_resid, 1)
                dve.wait_ge(ln_resid, n)
                nc.vector.tensor_scalar(f, vrr, -0.5, 1.5, ALU.mult, ALU.add).then_inc(ln_factor, 1)
                dve.wait_ge(ln_factor, n)
                nc.vector.tensor_tensor(rstd, r, f, ALU.mult).then_inc(ln_rstd, 1)

            def x_moments(i):
                dve.wait_ge(x_loaded[i], 16)
                if i:
                    dve.wait_ge(ln_rstd, i)
                row_stats(xs[:, i * PT:(i + 1) * PT, :], PT)
                dve.wait_ge(ln_stats, i + 1)
                moments(i + 1, mv0[:, i * PT:(i + 1) * PT, :], PT)

            def x_rstd(i):
                inverse_root(i + 1, rstd0[:, i * PT:(i + 1) * PT], PT)

            def hidden_rows(g):
                dve.wait_ge(z0_ready, g + 1)
                if g == 0:
                    dve.wait_ge(w_loaded, 16)
                nc.vector.scalar_tensor_tensor(
                    out=z0[g % 2][:], in0=z0[g % 2][:], scalar=0.0,
                    in1=w_all[:].unsqueeze(1).broadcast_to([P, TK, C]), op0=ALU.max, op1=ALU.mult,
                ).then_inc(w0_ready, 1)

            def low_turned(step):
                dve.wait_ge(at_hi, step.done())
                nc.vector.tensor_tensor(at[step.j % N_AT][:, 1], turn[step.j % 2][:], at[step.j % N_AT][:, 0],
                                        ALU.subtract).then_inc(at_lo, 1)

            def add_part(step):
                dve.wait_ge(spectral, step.done())
                if step.ran(1):
                    dve.wait_ge(summed, step.back(1).done())
                cols = spec[:, step.chunk * COLS:(step.chunk + 1) * COLS]
                nc.vector.tensor_tensor(cols, part[step.j % 2][:], cols, ALU.add).then_inc(summed, 1)

            def fold_product(last):
                dve.wait_ge(half_ready, last.blocks())
                nc.vector.tensor_tensor(fold[:], prod[last.parity][:, 0:ROWS], half[:], ALU.add
                                        ).then_inc(fold_ready, 1)

            def block_rows(row):
                return xs[:, row * TN:(row + 1) * TN, :] if isinstance(row, int) else xs[:, bass.ds(row * TN, TN), :]

            def add_rows(last, row):
                dve.wait_ge(rows_turned, last.blocks())
                rows = block_rows(row)
                nc.vector.tensor_tensor(rows, prod[last.parity][:, 0:ROWS].rearrange("p (t c) -> p t c", c=C),
                                        rows, ALU.add).then_inc(x_ready, 1)
                return rows

            def norm_block(rows):
                for i in range(TN):
                    last = nc.vector.tensor_scalar(z1[:, i, :], rows[:, i, :], mv1[:, i, 0:1], rstd1[:, i:i + 1],
                                                   ALU.subtract, ALU.mult)
                last.then_inc(z1_ready, 1)

            def low_h1(last):
                dve.wait_ge(h1_hi, last.blocks())
                nc.vector.scalar_tensor_tensor(out=h1[last.parity][:, 1], in0=z1[:], scalar=0.0,
                                               in1=h1[last.parity][:, 0], op0=ALU.max, op1=ALU.subtract
                                               ).then_inc(h1_lo, 1)

            def first_sweep(step, turning=True):
                ends = step.ran(CHUNKS)
                if step.chunk == 2 and ends:
                    fold_product(step.back(3))
                if step.chunk == 3 and ends:
                    last = step.back(4)
                    rows = add_rows(last, last.block())
                    dve.wait_ge(x_ready, last.blocks())
                if step.chunk == 4 and ends:
                    last = step.back(5)
                    inverse_root(last.blocks(X_PIECES + 1), rstd1[:], TN)
                    dve.wait_ge(ln_rstd, last.blocks(X_PIECES + 1))
                    norm_block(block_rows(last.block()))
                if step.chunk == 5 and ends:
                    low_h1(step.back(6))
                if turning:
                    low_turned(step)
                if step.chunk == 3 and ends:
                    row_stats(rows, TN)
                    dve.wait_ge(ln_stats, last.blocks(X_PIECES + 1))
                if step.ran(SPEC_LAG + 1):
                    add_part(step.back(SPEC_LAG + 1))
                if step.chunk == 3 and ends:
                    moments(last.blocks(X_PIECES + 1), mv1[:], TN)

            x_moments(0)
            x_rstd(0)
            for j in range(PAIR):
                if j % 2 == 0 and j // 2 + 1 < X_PIECES:
                    x_moments(j // 2 + 1)
                if j < CHUNKS:
                    hidden_rows(j)
                if j == SPEC_LAG + 1:
                    dve.wait_ge(spec_zeroed, 1)
                first_sweep(Step(j))
                if j % 2 == 0 and j // 2 + 1 < X_PIECES:
                    x_rstd(j // 2 + 1)
            with dve.Fori(1, PAIRS) as pair:
                q0, b0 = dve.snap(pair * PAIR), dve.snap(pair * 2)
                for j in range(PAIR):
                    first_sweep(Step(j, q0, b0))

            def split_spectrum(c):
                dve.wait_ge(sp_turned, c + 1)
                if c >= 2:
                    dve.wait_ge(sp_lo, c - 1)
                nc.vector.tensor_tensor(
                    z0[c % 2][:], prod[1][:].rearrange("p (t c) -> p t c", c=C),
                    coef[:, c * TK:(c + 1) * TK].unsqueeze(2).broadcast_to([P, TK, C]), ALU.mult,
                ).then_inc(sp_scaled, 1)
                dve.wait_ge(sp_hi, c + 1)
                nc.vector.tensor_tensor(wt[:, 1, c * TK:(c + 1) * TK, :], z0[c % 2][:],
                                        wt[:, 0, c * TK:(c + 1) * TK, :], ALU.subtract).then_inc(sp_lo, 1)

            for s in range(STEPS, TAIL_END):
                if s <= STEPS + SPEC_LAG:
                    first = Step(s)
                    if s < STEPS + 6:
                        first_sweep(first, turning=False)
                    else:
                        add_part(first.back(SPEC_LAG + 1))
                if 0 <= s - SP_TURN - 1 < CHUNKS:
                    split_spectrum(s - SP_TURN - 1)
                if s >= SWEEP2:
                    q = second(s)
                    if q.j >= STEPS + CHUNKS and q.chunk == 2:
                        fold_product(q.back(3))
                    if q.j >= STEPS + CHUNKS and q.chunk == 3:
                        add_rows(q.back(4), q.back(4).block() - 2)
                    low_turned(q)
            with dve.Fori(PAIRS + 1, 2 * PAIRS) as pair:
                q0, b0 = dve.snap(pair * PAIR), dve.snap(pair * 2)
                for j in range(PAIR):
                    q = Step(j, q0, b0)
                    if q.chunk == 2:
                        fold_product(q.back(3))
                    if q.chunk == 3:
                        last = q.back(4)
                        row = dve.snap((last.block() - 2) % BLOCKS)
                        add_rows(last, row)
                    low_turned(q)
            fold_product(Step(2 * STEPS - 1))
            add_rows(Step(2 * STEPS - 1), BLOCKS - 3)

        @block.tensor
        def _(pe):
            pe.wait_ge(ident_ready, 1)
            pe.wait_ge(ev_loaded, 16)
            nc.tensor.transpose(prod[1][:, 0:P], ev_rows, ident[:]).then_inc(ev_turned, 1)

            def turn_chunk(step, loads):
                slot, c = step.j % PAIR // 2, step.j % 2
                if loads is not None and c == 0:
                    pe.wait_ge(nat_loaded[slot], loads)
                if step.ran(2):
                    pe.wait_ge(at_lo, step.back(2).done())
                for k in range(TK):
                    for n in range(TN):
                        last = nc.tensor.transpose(turn[step.j % 2][:, k, n * P:(n + 1) * P],
                                                   nat[slot][:, n, c * COLS + k * P:c * COLS + (k + 1) * P], ident[:])
                last.then_inc(turned, 1)

            def project(step):
                pe.wait_ge(at_lo, step.done())
                bank, a = prod[step.parity], at[step.j % N_AT]
                if step.chunk == 0 and step.ran(2 * CHUNKS):
                    pe.wait_ge(x_ready, step.blocks(-1))
                for k in range(TK):
                    n = step.chunk * TK + k
                    nc.tensor.matmul(bank[:], wt[:, 0, n, :], a[:, :, k, :], start=(n == 0), stop=False,
                                     skip_group_check=True)
                    last = nc.tensor.matmul(bank[:, 0:ROWS], wt[:, 1, n, :], a[:, 0, k, :], start=False,
                                            stop=(n == NT - 1), skip_group_check=True)
                last.then_inc(projected, 1)

            def spectrum_part(step):
                pe.wait_ge(nat_lo, step.done())
                if step.ran(2):
                    pe.wait_ge(summed, step.back(2).done())
                if step.chunk == 0:
                    pe.wait_ge(h1_lo, step.blocks())
                h, a, bank = h1[step.parity], nsp[step.j % N_NAT], part[step.j % 2]
                for n in range(TN):
                    nc.tensor.matmul(bank[:], h[:, 0, n, :], a[:, 0, n, :], start=(n == 0), stop=False)
                    nc.tensor.matmul(bank[:], h[:, 0, n, :], a[:, 1, n, :], start=False, stop=False)
                    last = nc.tensor.matmul(bank[:], h[:, 1, n, :], a[:, 0, n, :], start=False, stop=(n == TN - 1))
                last.then_inc(spectral, 1)

            def turn_rows(last_step):
                pe.wait_ge(fold_ready, last_step.blocks())
                for n in range(TN):
                    last = nc.tensor.transpose(prod[last_step.parity][:, n * P:(n + 1) * P],
                                               fold[:, n * P:(n + 1) * P], ident[:])
                last.then_inc(rows_turned, 1)

            def first_sweep(step, loads):
                turn_chunk(step, loads)
                if step.ran(TURN_LAG):
                    q = step.back(TURN_LAG)
                    if isinstance(step.q0, int) and q.j < CHUNKS:
                        pe.wait_ge(w0_lo, q.j + 1)
                    if q.j == CHUNKS and isinstance(step.q0, int):
                        pe.wait_ge(coef_ready, 1)
                    project(q)
                if step.ran(SPEC_LAG):
                    spectrum_part(step.back(SPEC_LAG))
                if step.chunk == 2 and step.ran(CHUNKS):
                    turn_rows(step.back(3))

            for j in range(PAIR):
                first_sweep(Step(j), 16)
            with pe.Fori(1, PAIRS) as pair:
                q0, b0 = pe.snap(pair * PAIR), pe.snap(pair * 2)
                loads = pe.snap(q0 + 16)
                for j in range(PAIR):
                    first_sweep(Step(j, q0, b0), loads)

            for s in range(STEPS, TAIL_END):
                if s >= SWEEP2:
                    turn_chunk(second(s), None)
                if s < STEPS + TURN_LAG:
                    project(Step(s - TURN_LAG))
                if s >= SWEEP2 + TURN_LAG:
                    q = second(s).back(TURN_LAG)
                    if q.j < STEPS + CHUNKS:
                        pe.wait_ge(sp_lo, q.j - STEPS + 1)
                    project(q)
                if s < STEPS + SPEC_LAG:
                    spectrum_part(Step(s - SPEC_LAG))
                if s == STEPS + 2:
                    turn_rows(Step(s - 3))
                c = s - SP_TURN
                if 0 <= c < CHUNKS:
                    pe.wait_ge(summed, STEPS - CHUNKS + c + 1)
                    if c == 0:
                        pe.wait_ge(x_ready, BLOCKS)
                    else:
                        pe.wait_ge(sp_scaled, c)
                    for k in range(TK):
                        last = nc.tensor.transpose(prod[1][:, k * P:(k + 1) * P],
                                                   spec[:, c * COLS + k * P:c * COLS + (k + 1) * P], ident[:])
                    last.then_inc(sp_turned, 1)
                if s >= SWEEP2 and second(s).j == STEPS + CHUNKS + 2:
                    turn_rows(second(s).back(3))
            with pe.Fori(PAIRS + 1, 2 * PAIRS) as pair:
                q0, b0 = pe.snap(pair * PAIR), pe.snap(pair * 2)
                for j in range(PAIR):
                    q = Step(j, q0, b0)
                    turn_chunk(q, q0)
                    project(q.back(TURN_LAG))
                    if q.chunk == 2:
                        turn_rows(q.back(3))
            project(Step(2 * STEPS - 2))
            project(Step(2 * STEPS - 1))
            turn_rows(Step(2 * STEPS - 1))


_INS = ['x', 'adj', 'L0_gnn_W', 'L1_gnn_evals', 'L1_gnn_t']
_OUTS = [((4096, 128), 'float32')]


def kernel(**inputs):
    import numpy as _np
    import concourse.bacc as _bacc
    from concourse import mybir as _mybir
    from concourse.bass_utils import run_bass_kernel_spmd as _run

    nc = _bacc.Bacc("TRN2", target_bir_lowering=False, num_devices=1)
    arrays, args = {}, []
    for name in _INS:
        a = _np.ascontiguousarray(inputs[name])
        arrays[f"in_{name}_dram"] = a
        args.append(nc.dram_tensor(f"in_{name}_dram", a.shape, _mybir.dt.from_np(a.dtype), kind="ExternalInput").ap())
    for i, (shape, dtype) in enumerate(_OUTS):
        dt = _mybir.dt.from_np(_np.dtype(dtype))
        args.append(nc.dram_tensor(f"out_{i}_dram", shape, dt, kind="ExternalOutput").ap())
    program(nc, *args)
    r = _run(nc, [arrays], core_ids=[0])
    return r.results[0]["out_0_dram"]
```

```python
from contextlib import ExitStack

import concourse.bass as bass
from concourse import mybir

F32 = mybir.dt.float32
F32R = mybir.dt.float32r
ALU = mybir.AluOpType
ACT = mybir.ActivationFunctionType

P = 128
TN = 2
ROWS = TN * P
TK = 4
COLS = TK * P
EPS = 1e-5
T_MIN = 1e-8
N_AT = 3
N_NAT = 4
TURN_LAG = 2
SPEC_LAG = 13
SPLIT_LAG = 11
Q = 32
WIDE = 2 * COLS
ORDER = ((0, 0), (1, 0), (0, 1), (1, 1), (2, 0), (3, 0), (2, 1), (3, 1))
BY_PE_1 = (0, 2, 4, 6)
BY_VECTOR_1 = (1, 3, 5, 7)
BY_PE = (4, 6)
BY_VECTOR = (0, 1, 2, 3, 5, 7)
LO_VECTOR = (3, 4, 6)
LO_POOL = (0, 1, 2, 5, 7)
HI_ORDER = (0, 1, 2, 3, 4, 5, 7, 6)


class Step:

    def __init__(self, j, q0=0, b0=0):
        self.j, self.q0, self.b0 = j, q0, b0

    def back(self, n):
        return Step(self.j - n, self.q0, self.b0)

    def ran(self, n):
        return not isinstance(self.q0, int) or self.j >= n

    def done(self):
        return self.q0 + (self.j + 1)

    def block(self):
        return self.b0 + self.j // 8

    def blocks(self, n=1):
        return self.b0 + (self.j // 8 + n)

    @property
    def chunk(self):
        return self.j % 8

    @property
    def parity(self):
        return self.j // 8 % 2

    @property
    def wide(self):
        return ORDER[self.chunk][0]

    @property
    def half(self):
        return ORDER[self.chunk][1]

    @property
    def slot(self):
        return self.parity * 4 + self.wide

    @property
    def tiles(self):
        return (2 * self.wide + self.half) * TK

    @property
    def at_slot(self):
        j = self.j % 16
        return 1 if j == 15 else j % N_AT

    @property
    def before(self):
        return next(n for n in range(1, 16) if self.back(n).at_slot == self.at_slot)


def second_half(wide):
    return ORDER.index((wide, 1))


def program(nc, x, adj, w0, evals, t, out):
    N, C = x.shape
    NT = N // P
    BLOCKS = N // ROWS
    CHUNKS = N // COLS
    STEPS = BLOCKS * CHUNKS
    PAIR = 2 * CHUNKS
    PAIRS = STEPS // PAIR
    assert C == P and CHUNKS == 8 and BLOCKS % 2 == 0
    X_PIECES = 4
    PT = NT // X_PIECES

    with ExitStack() as ctx:
        def sb(name, shape, dt=F32):
            return ctx.enter_context(nc.sbuf_tensor(name, shape, dt))

        def psum(name, shape):
            return ctx.enter_context(nc.psum_tensor(name, shape, F32))

        def sem(name):
            return ctx.enter_context(nc.semaphore(name))

        nat = [sb(f"nat{i}", [P, TN, 2 * COLS]) for i in range(PAIR // 2)]
        at = [sb(f"at{i}", [P, 2, TK, ROWS], F32R) for i in range(N_AT)]
        nsp = [sb(f"nsp{i}", [P, 2, TN, COLS], F32R) for i in range(N_NAT)]
        wt = sb("wt", [P, 2, NT, C], F32R)
        h1_all = sb("h1_all", [P, 2 * TK * ROWS], F32R)
        h1 = [h1_all[:, i * 2 * ROWS:(i + 1) * 2 * ROWS].rearrange("p (h n c) -> p h n c", h=2, n=TN)
              for i in range(2)]
        xs = sb("xs", [P, NT, C])
        spec = sb("spec", [P, N])
        xp = spec[:].rearrange("p (n c) -> p n c", c=C)
        quad = [sb(f"quad{i}", [P, ROWS // Q, TK * Q]) for i in range(2)]
        raw = [spec[:, i * TK * ROWS:(i + 1) * TK * ROWS].rearrange("p (k n) -> p k n", k=TK)
               for i in range(4)]
        h1_turned = h1_all[:].rearrange("p (h k r) -> p h k r", h=2, k=TK)
        nsp_turned = [t_[:].rearrange("p h n (k r) -> p h (n k) r", r=ROWS) for t_ in nsp]
        at2 = nsp_turned + [at[0][:], h1_turned, at[2][:], at[1][:]]
        ident = sb("ident", [P, P])
        half = sb("half", [P, ROWS])
        w_all = half[:, 0:C]
        fold = sb("fold", [P, ROWS])
        z1 = fold[:].rearrange("p (n c) -> p n c", c=C)
        z0_all = sb("z0_all", [P, 2 * TK * C])
        z0 = [z0_all[:, i * TK * C:(i + 1) * TK * C].rearrange("p (k c) -> p k c", c=C)
              for i in range(2)]
        raw1 = z0_all[:].rearrange("p (k n) -> p k n", k=TK)
        stats = sb("stats", [P, PT, 6])
        mv0 = sb("mv0", [P, NT, 2])
        mv1 = sb("mv1", [P, TN, 2])
        rstd0 = sb("rstd0", [P, NT])
        shift0 = sb("shift0", [P, NT])
        rstd1 = sb("rstd1", [P, TN])
        lnv = sb("lnv", [P, 6, PT])
        tneg = sb("tneg", [P, 1])
        coef = sb("coef", [P, NT])

        turn = [psum(f"turn{i}", [P, TK, ROWS]) for i in range(2)]
        prod = [psum(f"prod{i}", [P, 2 * ROWS]) for i in range(2)]
        part = [psum(f"part{i}", [P, COLS]) for i in range(2)]

        x_loaded = [sem(f"x_loaded{i}") for i in range(X_PIECES)]
        w_loaded, t_loaded, ev_loaded = sem("w_loaded"), sem("t_loaded"), sem("ev_loaded")
        xs_loaded = sem("xs_loaded")
        quad_loaded = [sem(f"quad_loaded{i}") for i in range(2)]
        nat_loaded = [sem(f"nat_loaded{i}") for i in range(PAIR // 2)]
        stored = sem("stored")
        zeroed, ident_ready = sem("zeroed"), sem("ident_ready")
        spec_zeroed = sem("spec_zeroed")
        t_ready, coef_ready = sem("t_ready"), sem("coef_ready")
        raw_turned = sem("raw_turned")
        turned, at_hi, vector_lo, projected = sem("turned"), sem("at_hi"), sem("vector_lo"), sem("projected")
        nat_hi, pool_lo, spectral, summed = sem("nat_hi"), sem("pool_lo"), sem("spectral"), sem("summed")
        half_ready, fold_ready, rows_turned = sem("half_ready"), sem("fold_ready"), sem("rows_turned")
        x_ready, z1_ready = sem("x_ready"), sem("z1_ready")
        h1_hi, h1_lo = sem("h1_hi"), sem("h1_lo")
        ln_stats, ln_moments, ln_var, ln_sqrt = sem("ln_stats"), sem("ln_moments"), sem("ln_var"), sem("ln_sqrt")
        ln_recip, ln_square, ln_resid, ln_factor = sem("ln_recip"), sem("ln_square"), sem("ln_resid"), sem("ln_factor")
        ln_rstd, ln_shift = sem("ln_rstd"), sem("ln_shift")
        z0_ready, w0_ready, w0_hi, w0_lo = sem("z0_ready"), sem("w0_ready"), sem("w0_hi"), sem("w0_lo")
        sp_turned, sp_scaled, sp_hi, sp_lo = sem("sp_turned"), sem("sp_scaled"), sem("sp_hi"), sem("sp_lo")

        adj_v = adj.rearrange("(b t p) k -> b p t k", t=TN, p=P)
        out_v = out.rearrange("(b t p) c -> b p t c", t=TN, p=P)
        adj_q = adj.rearrange("(b n r) (m g f) -> b m g r n f", n=ROWS // Q, r=Q, g=P // Q, f=WIDE // 4)
        x_v = x.rearrange("(t p) c -> p t c", p=P)
        adj_c = adj.rearrange("(b n r) (m g f) -> b m g r n f", n=ROWS // Q, r=Q, g=P // Q, f=COLS // 4)
        x_wide = x.rearrange("(m h p j) c -> m p h (j c)", h=2, p=P, j=TK)
        SP_TURN = STEPS + SPEC_LAG + 3 - CHUNKS
        SWEEP2 = SP_TURN
        TAIL_END = SWEEP2 + PAIR

        def second(s):
            return Step(STEPS + s - SWEEP2)

        def wt_group(part, c):
            n = Step(c).tiles
            return wt[:, part, n:n + TK, :]

        def ordered(columns, half, k):
            return columns.rearrange("p (q j) -> p j q", q=P)[:, half * TK + k]

        def ordered_1(columns, half, k):
            return columns[:, half * COLS:(half + 1) * COLS].rearrange("p (q j) -> p j q", q=P)[:, k]

        def turned_by_pe_1(b, c):
            return b * len(BY_PE_1) + (CHUNKS - len(BY_PE_1) + BY_PE_1.index(c) + 1)

        def turned_by_vector_1(b, c):
            return b * len(BY_VECTOR_1) + (BY_VECTOR_1.index(c) + 1 - len(BY_VECTOR_1))

        TURNED_1 = turned_by_pe_1(BLOCKS - 1, BY_PE_1[-1])
        RAW_1 = turned_by_vector_1(BLOCKS - 1, BY_VECTOR_1[-1])

        STAYED = 2

        def turned_stayed(q):
            return TURNED_1 + q.j - STEPS + 1

        def turned_by_pe(b, c):
            return (b - (BLOCKS + STAYED)) * len(BY_PE) + (TURNED_1 + STAYED * CHUNKS + BY_PE.index(c) + 1)

        def turned_by_vector(b, c):
            return (b - (BLOCKS + STAYED)) * len(BY_VECTOR) + (RAW_1 + BY_VECTOR.index(c) + 1)

        def split(b, c):
            if c in LO_VECTOR:
                return vector_lo, ((b - (BLOCKS + STAYED)) * len(LO_VECTOR)
                                   + (STEPS + STAYED * CHUNKS + LO_VECTOR.index(c) + 1))
            return pool_lo, (b - (BLOCKS + STAYED)) * len(LO_POOL) + (STEPS + LO_POOL.index(c) + 1)

        def hi_done(q):
            return q.q0 + (q.j - q.chunk + HI_ORDER.index(q.chunk) + 1)

        def raw_use(j):
            uses = [8 * i + c for i in range(-2, 2) for c in BY_VECTOR]
            n = uses.index(j)
            return raw[(n - 2 * len(BY_VECTOR)) % 4], uses[n - 4]

        block = ctx.enter_context(nc.Block())

        @block.sync
        def _(sp):
            def load(slot, source_block, m):
                sp.dma_start(nat[slot][:], adj_v[source_block, :, :, m * WIDE:(m + 1) * WIDE]
                             ).then_inc(nat_loaded[slot], 16)

            def load_quad(tile, source_block, m, loaded):
                for g in range(P // Q):
                    sp.dma_start(tile[g * Q:(g + 1) * Q], adj_q[source_block, m, g]).then_inc(loaded, 16)

            def load_x(i):
                sp.dma_start(spec[:, i * PT * C:(i + 1) * PT * C].rearrange("p (h f) -> p h f", h=2), x_wide[i]
                             ).then_inc(x_loaded[i], 16)

            def load_again(source_block, c):
                n, chunk = c // 2 % 2, Step(c)
                for g in range(P // Q):
                    sp.dma_start(quad[n][g * Q:(g + 1) * Q], adj_c[source_block, 2 * chunk.wide + chunk.half, g]
                                 ).then_inc(quad_loaded[n], 16)

            load_x(0)
            load_x(1)
            load(0, 0, 0)
            load_x(2)
            load(1, 0, 1)
            load_x(3)
            load(2, 0, 2)
            load(3, 0, 3)
            load(4, 1, 0)
            sp.dma_start(xs[:], x_v).then_inc(xs_loaded, 16)
            load(5, 1, 1)
            load_again(1, 1)
            load(6, 1, 2)
            load_again(1, 3)
            load(7, 1, 3)
            for c in (5, 7):
                sp.wait_ge(raw_turned, turned_by_vector_1(1, c - 4))
                load_again(1, c)
            with sp.Fori(1, PAIRS) as pair:
                q0, b0 = sp.snap(pair * PAIR), sp.snap(pair * 2)
                quad_free = [{c: sp.snap(turned_by_vector_1(b0 + (i + c // 4 - 1), (c + 4) % CHUNKS))
                              for c in BY_VECTOR_1} for i in range(2)]
                for i in range(2):
                    def load_own(m):
                        sp.wait_ge(pool_lo, Step(i * CHUNKS + 2 * m + 1, q0, b0).back(PAIR).done())
                        load(i * 4 + m, b0 + i, m)

                    for c in BY_VECTOR_1:
                        load_own(c // 2)
                        sp.wait_ge(raw_turned, quad_free[i][c])
                        load_again(b0 + i, c)

            def load_second(b, m, parity, source_block):
                slot = parity * 4 + m
                if second_half(m) in BY_PE:
                    load(slot, source_block, m)
                else:
                    tile = nat[slot][:].rearrange("p t k -> p (t k)").rearrange("p (n f) -> p n f", n=ROWS // Q)
                    load_quad(tile, source_block, m, nat_loaded[slot])

            def store(b, place):
                sp.wait_ge(x_ready, b + 1)
                rows = xs[:, place * TN:(place + 1) * TN, :] if isinstance(place, int) else \
                    xs[:, bass.ds(place * TN, TN), :]
                sp.dma_start(out_v[place], rows).then_inc(stored, 16)

            for b in range(BLOCKS + STAYED, BLOCKS + 2 * STAYED):
                for m in range(4):
                    sp.wait_ge(turned, turned_stayed(Step((b - STAYED) * CHUNKS + second_half(m))))
                    load_second(b, m, b % 2, b - (BLOCKS + STAYED))
            store(BLOCKS, BLOCKS - 2)
            with sp.Fori(PAIRS + 2, 2 * PAIRS) as pair:
                b0 = sp.snap(pair * 2)
                source = sp.snap(b0 - (BLOCKS + 2))
                places = [sp.snap((b0 + (i - 5)) % BLOCKS) for i in range(2)]
                for i in range(2):
                    for m in range(4):
                        c = second_half(m)
                        if c in BY_PE:
                            sp.wait_ge(turned, turned_by_pe(b0 + (i - 2), c))
                        else:
                            sp.wait_ge(raw_turned, turned_by_vector(b0 + (i - 2), c))
                        load_second(b0 + i, m, i, source + i)
                    store(b0 + (i - 3), places[i])
            for b in range(2 * BLOCKS - 3, 2 * BLOCKS):
                store(b, b - (BLOCKS + STAYED))
            sp.wait_ge(stored, 16 * BLOCKS)

        @block.gpsimd
        def _(pool):
            nc.gpsimd.memset(ident[:], 0.0).then_inc(zeroed, 1)
            pool.wait_ge(zeroed, 1)
            nc.gpsimd.affine_select(out=ident[:], in_=ident[:], compare_op=ALU.not_equal, fill=1.0, base=0,
                                    pattern=[[-1, P]], channel_multiplier=1).then_inc(ident_ready, 1)

            def hidden_rows(g):
                pool.wait_ge(z0_ready, g + 1)
                if g == 0:
                    pool.wait_ge(w_loaded, 16)
                n = Step(g).tiles
                nc.gpsimd.tensor_tensor(xp[:, n:n + TK, :], xp[:, n:n + TK, :],
                                        w_all.unsqueeze(1).broadcast_to([P, TK, C]), ALU.mult).then_inc(w0_ready, 1)

            def low_rows(g):
                pool.wait_ge(w0_hi, g + 1)
                n = Step(g).tiles
                nc.gpsimd.tensor_tensor(wt_group(1, g), xp[:, n:n + TK, :], wt_group(0, g), ALU.subtract
                                        ).then_inc(w0_lo, 1)

            def low_nat(step):
                pool.wait_ge(nat_hi, step.done())
                slot, c = step.j % PAIR // 2, step.j % 2
                nc.gpsimd.tensor_tensor(nsp[step.j % N_NAT][:, 1], nat[slot][:, :, c * COLS:(c + 1) * COLS],
                                        nsp[step.j % N_NAT][:, 0], ALU.subtract).then_inc(pool_lo, 1)

            hidden_rows(0)
            for j in range(PAIR):
                if j + 1 < CHUNKS:
                    hidden_rows(j + 1)
                if j < CHUNKS:
                    low_rows(j)
                if j == CHUNKS:
                    pool.wait_ge(w0_lo, CHUNKS)
                    nc.gpsimd.memset(spec[:], 0.0).then_inc(spec_zeroed, 1)
                if j >= SPLIT_LAG:
                    low_nat(Step(j - SPLIT_LAG))
            with pool.Fori(1, PAIRS) as pair:
                q0 = pool.snap(pair * PAIR)
                for j in range(PAIR):
                    low_nat(Step(j, q0).back(SPLIT_LAG))
            for s in range(STEPS, STEPS + SPLIT_LAG):
                low_nat(Step(s - SPLIT_LAG))

            with pool.Fori(PAIRS + 1, 2 * PAIRS) as pair:
                q0, b0 = pool.snap(pair * PAIR), pool.snap(pair * 2)
                for i in range(2):
                    for c in LO_POOL:
                        q = Step(i * CHUNKS + c, q0, b0)
                        pool.wait_ge(at_hi, hi_done(q))
                        nc.gpsimd.tensor_tensor(at2[c][:, 1], raw_use(q.j)[0], at2[c][:, 0], ALU.subtract
                                                ).then_inc(pool_lo, 1)

        @block.scalar
        def _(act):
            act.dma_start(tneg[:], t.rearrange("(a b) -> a b", a=1).partition_broadcast(P)
                          ).then_inc(t_loaded, 16)
            act.dma_start(coef[:].rearrange("p (m j) -> p m j", j=WIDE // P),
                          evals.rearrange("(m p j) -> p m j", p=P, j=WIDE // P)).then_inc(ev_loaded, 16)
            act.dma_start(w_all, w0.rearrange("(a b) -> a b", a=1).partition_broadcast(P)
                          ).then_inc(w_loaded, 16)
            act.wait_ge(t_ready, 1)
            act.wait_ge(ev_loaded, 16)
            nc.scalar.activation(coef[:], coef[:], ACT.Exp, scale=tneg[:, 0:1]).then_inc(coef_ready, 1)

            def root(n, tiles):
                act.wait_ge(ln_var, n)
                nc.scalar.activation(lnv[:, 1, 0:tiles], lnv[:, 0, 0:tiles], ACT.Sqrt).then_inc(ln_sqrt, 1)

            def relu_rows(g):
                if Step(g).half == 0:
                    act.wait_ge(ln_shift, Step(g).wide + 1)
                for i in range(TK):
                    n = Step(g).tiles + i
                    last = nc.scalar.activation(xp[:, n, :], xp[:, n, :], ACT.Relu,
                                                bias=shift0[:, n:n + 1], scale=rstd0[:, n:n + 1])
                last.then_inc(z0_ready, 1)

            def high_rows(g):
                act.wait_ge(w0_ready, g + 1)
                n = Step(g).tiles
                nc.scalar.activation(wt_group(0, g), xp[:, n:n + TK, :], ACT.Copy).then_inc(w0_hi, 1)

            def high_turned(step, sweep=1):
                c = step.chunk
                source = turn[c % 2][:]
                if sweep == 2:
                    act.wait_ge(turned, turned_stayed(step))
                elif isinstance(step.q0, int) and step.j < CHUNKS:
                    act.wait_ge(turned, step.done())
                elif c in BY_PE_1:
                    act.wait_ge(turned, turned_by_pe_1(step.block(), c))
                    source = turn[BY_PE_1.index(c) % 2][:]
                else:
                    act.wait_ge(raw_turned, turned_by_vector_1(step.block(), c))
                    source = raw1
                if step.ran(step.before):
                    act.wait_ge(projected, step.back(step.before).done())
                nc.scalar.activation(at[step.at_slot][:, 0], source, ACT.Copy).then_inc(at_hi, 1)

            def high_nat(step):
                slot, c = step.j % PAIR // 2, step.j % 2
                if c == 0:
                    act.wait_ge(nat_loaded[slot], step.q0 + (step.j // PAIR + 1) * 16)
                if step.ran(N_NAT):
                    act.wait_ge(spectral, step.back(N_NAT).done())
                nc.scalar.activation(nsp[step.j % N_NAT][:, 0], nat[slot][:, :, c * COLS:(c + 1) * COLS],
                                     ACT.Copy).then_inc(nat_hi, 1)

            def copy_half(last):
                act.wait_ge(projected, last.done())
                if last.ran(CHUNKS):
                    act.wait_ge(fold_ready, last.blocks(0))
                nc.scalar.activation(half[:], prod[last.parity][:, ROWS:2 * ROWS], ACT.Copy
                                     ).then_inc(half_ready, 1)

            def high_h1(last):
                act.wait_ge(z1_ready, last.blocks())
                nc.scalar.activation(h1[last.parity][:, 0], z1, ACT.Relu).then_inc(h1_hi, 1)

            def first_sweep(step, turning=True):
                if step.chunk == 2 and step.ran(CHUNKS):
                    copy_half(step.back(3))
                ends = step.ran(CHUNKS)
                if step.ran(SPLIT_LAG):
                    high_nat(step.back(SPLIT_LAG))
                if step.chunk == 4 and ends:
                    root(step.back(5).blocks(X_PIECES + 1), TN)
                if turning:
                    high_turned(step)
                if step.chunk == 4 and ends:
                    high_h1(step.back(5))

            root(1, PT)
            relu_rows(0)
            root(2, PT)
            for j in range(PAIR):
                if j + 1 < CHUNKS:
                    relu_rows(j + 1)
                if j < CHUNKS:
                    high_rows(j)
                first_sweep(Step(j))
                if j + 3 <= X_PIECES:
                    root(j + 3, PT)
            with act.Fori(1, PAIRS) as pair:
                q0, b0 = act.snap(pair * PAIR), act.snap(pair * 2)
                for j in range(PAIR):
                    first_sweep(Step(j, q0, b0))

            def high_spectrum(c):
                act.wait_ge(sp_scaled, c + 1)
                nc.scalar.activation(wt_group(0, c), z0[c % 2], ACT.Copy).then_inc(sp_hi, 1)

            for s in range(STEPS, TAIL_END):
                if s < STEPS + SPLIT_LAG:
                    if s == STEPS + 2:
                        copy_half(Step(s).back(3))
                    high_nat(Step(s - SPLIT_LAG))
                    if s == STEPS + 4:
                        root(Step(s).back(5).blocks(X_PIECES + 1), TN)
                        high_h1(Step(s).back(5))
                if 0 <= s - SP_TURN - 1 < CHUNKS:
                    high_spectrum(s - SP_TURN - 1)
                if s >= SWEEP2:
                    q = second(s)
                    if q.chunk == 2 and q.j >= STEPS + CHUNKS:
                        copy_half(q.back(3))
                    high_turned(q, sweep=2)
            with act.Fori(PAIRS + 1, 2 * PAIRS) as pair:
                q0, b0 = act.snap(pair * PAIR), act.snap(pair * 2)
                for j in [i * CHUNKS + c for i in range(2) for c in HI_ORDER]:
                    q = Step(j, q0, b0)
                    c = q.chunk
                    act.wait_ge(projected, q.back(CHUNKS).done())
                    if c in BY_PE:
                        act.wait_ge(turned, turned_by_pe(q.block(), c))
                        source = turn[BY_PE.index(c)][:]
                    else:
                        act.wait_ge(raw_turned, turned_by_vector(q.block(), c))
                        source = raw_use(j)[0]
                    nc.scalar.activation(at2[c][:, 0], source, ACT.Copy).then_inc(at_hi, 1)
                    if c == 3:
                        copy_half(q.back(4))
            copy_half(Step(2 * STEPS - 1))

        @block.vector
        def _(dve):
            dve.wait_ge(t_loaded, 16)
            nc.vector.tensor_scalar(tneg[:], tneg[:], T_MIN, -1.0, ALU.max, ALU.mult).then_inc(t_ready, 1)

            def row_stats(rows, tiles):
                for i in range(tiles):
                    last = nc.vector.bn_stats(stats[:, i, :], rows[:, i, :])
                last.then_inc(ln_stats, 1)

            def moments(n, mv, tiles):
                for i in range(tiles):
                    last = nc.vector.bn_aggr(mv[:, i, :], stats[:, i, :])
                last.then_inc(ln_moments, 1)
                dve.wait_ge(ln_moments, n)
                nc.vector.tensor_scalar(lnv[:, 0, 0:tiles], mv[:, :, 1], EPS, None, ALU.add).then_inc(ln_var, 1)

            def inverse_root(n, rstd, tiles):
                v, root, r, rr, vrr, f = (lnv[:, i, 0:tiles] for i in range(6))
                dve.wait_ge(ln_sqrt, n)
                nc.vector.reciprocal(r, root).then_inc(ln_recip, 1)
                dve.wait_ge(ln_recip, n)
                nc.vector.tensor_tensor(rr, r, r, ALU.mult).then_inc(ln_square, 1)
                dve.wait_ge(ln_square, n)
                nc.vector.tensor_tensor(vrr, rr, v, ALU.mult).then_inc(ln_resid, 1)
                dve.wait_ge(ln_resid, n)
                nc.vector.tensor_scalar(f, vrr, -0.5, 1.5, ALU.mult, ALU.add).then_inc(ln_factor, 1)
                dve.wait_ge(ln_factor, n)
                nc.vector.tensor_tensor(rstd, r, f, ALU.mult).then_inc(ln_rstd, 1)
                dve.wait_ge(ln_rstd, n)

            def x_moments(i):
                dve.wait_ge(x_loaded[i], 16)
                row_stats(xp[:, i * PT:(i + 1) * PT, :], PT)
                dve.wait_ge(ln_stats, i + 1)
                moments(i + 1, mv0[:, i * PT:(i + 1) * PT, :], PT)

            def x_rstd(i):
                piece = slice(i * PT, (i + 1) * PT)
                inverse_root(i + 1, rstd0[:, piece], PT)
                nc.vector.scalar_tensor_tensor(out=shift0[:, piece], in0=mv0[:, piece, 0], scalar=-1.0,
                                               in1=rstd0[:, piece], op0=ALU.mult, op1=ALU.mult).then_inc(ln_shift, 1)

            def by_vector_1(step):
                return step.chunk in BY_VECTOR_1 and step.ran(CHUNKS)

            def low_turned(step, sweep=1):
                dve.wait_ge(at_hi, step.done())
                if sweep == 2 or not step.ran(CHUNKS):
                    source = turn[step.chunk % 2][:]
                else:
                    source = raw1 if by_vector_1(step) else turn[BY_PE_1.index(step.chunk) % 2][:]
                nc.vector.tensor_tensor(at[step.at_slot][:, 1], source, at[step.at_slot][:, 0],
                                        ALU.subtract).then_inc(vector_lo, 1)

            def turn_tile(tile, half, buffer):
                chunk = tile.rearrange("p n (i j) -> p j n i", i=Q)[:, half * TK:(half + 1) * TK]
                nc.vector.transpose(buffer.rearrange("p k (n r) -> p k n r", r=Q), chunk).then_inc(raw_turned, 1)

            def turn_on_vector_1(step):
                c = step.chunk
                n = c // 2 % 2
                dve.wait_ge(quad_loaded[n], step.block() * 128 + (c // 4 - 1) * 64)
                dve.wait_ge(vector_lo, step.back(2).done())
                turn_tile(quad[n][:], 0, raw1)

            def add_part(step, halves=(0, 1)):
                if 0 in halves:
                    dve.wait_ge(spectral, step.done())
                    if step.ran(1):
                        dve.wait_ge(summed, step.back(1).done())
                columns = slice(halves[0] * COLS // 2, (halves[-1] + 1) * COLS // 2)
                cols = spec[:, step.chunk * COLS:(step.chunk + 1) * COLS][:, columns]
                last = nc.vector.tensor_tensor(cols, part[step.j % 2][:, columns], cols, ALU.add)
                if 1 in halves:
                    last.then_inc(summed, 1)

            def fold_product(last, sweep=1):
                if sweep == 1 and last.ran(CHUNKS):
                    dve.wait_ge(h1_lo, last.blocks(0))
                dve.wait_ge(half_ready, last.blocks())
                nc.vector.tensor_tensor(fold[:], prod[last.parity][:, 0:ROWS], half[:], ALU.add
                                        ).then_inc(fold_ready, 1)

            def block_rows(row):
                return xs[:, row * TN:(row + 1) * TN, :] if isinstance(row, int) else xs[:, bass.ds(row * TN, TN), :]

            def add_rows(last, row):
                dve.wait_ge(rows_turned, last.blocks())
                rows = block_rows(row)
                nc.vector.tensor_tensor(rows, prod[last.parity][:, 0:ROWS].rearrange("p (t c) -> p t c", c=C),
                                        rows, ALU.add).then_inc(x_ready, 1)
                return rows

            def norm_block(rows):
                for i in range(TN):
                    last = nc.vector.tensor_scalar(z1[:, i, :], rows[:, i, :], mv1[:, i, 0:1], rstd1[:, i:i + 1],
                                                   ALU.subtract, ALU.mult)
                last.then_inc(z1_ready, 1)

            def low_h1(last):
                dve.wait_ge(h1_hi, last.blocks())
                nc.vector.scalar_tensor_tensor(out=h1[last.parity][:, 1], in0=z1, scalar=0.0,
                                               in1=h1[last.parity][:, 0], op0=ALU.max, op1=ALU.subtract
                                               ).then_inc(h1_lo, 1)

            def first_sweep(step, turning=True):
                ends = step.ran(CHUNKS)

                def turn_next():
                    if turning and by_vector_1(step.back(-1)):
                        turn_on_vector_1(step.back(-1))

                def add(halves=(0, 1)):
                    if step.ran(SPEC_LAG + 1):
                        add_part(step.back(SPEC_LAG + 1), halves)

                if step.chunk != 3:
                    add()
                if step.chunk == 3 and ends:
                    last = step.back(4)
                    n = last.blocks(X_PIECES + 1)
                    if isinstance(step.q0, int) and step.j < PAIR:
                        dve.wait_ge(xs_loaded, 16)
                    rows = add_rows(last, last.block())
                    dve.wait_ge(x_ready, last.blocks())
                    add(halves=(0,))
                    row_stats(rows, TN)
                    dve.wait_ge(ln_stats, n)
                    add(halves=(1,))
                    moments(n, mv1[:], TN)
                    if turning:
                        low_turned(step)
                elif step.chunk == 4 and ends:
                    last = step.back(5)
                    inverse_root(last.blocks(X_PIECES + 1), rstd1[:], TN)
                    norm_block(block_rows(last.block()))
                    if turning:
                        low_turned(step)
                    low_h1(last)
                    turn_next()
                else:
                    if step.chunk == 2 and ends:
                        fold_product(step.back(3))
                    if turning:
                        low_turned(step)
                    turn_next()

            x_moments(0)
            x_rstd(0)
            x_moments(1)
            x_rstd(1)
            x_moments(2)
            for j in range(PAIR):
                if j == SPEC_LAG + 1:
                    dve.wait_ge(spec_zeroed, 1)
                first_sweep(Step(j))
                if j + 2 < X_PIECES:
                    x_rstd(j + 2)
                if j + 3 < X_PIECES:
                    x_moments(j + 3)
            with dve.Fori(1, PAIRS) as pair:
                q0, b0 = dve.snap(pair * PAIR), dve.snap(pair * 2)
                for j in range(PAIR):
                    first_sweep(Step(j, q0, b0))

            def split_spectrum(c):
                dve.wait_ge(sp_turned, c + 1)
                if c >= 2:
                    dve.wait_ge(sp_lo, c - 1)
                if c == 0:
                    dve.wait_ge(coef_ready, 1)
                    dve.wait_ge(vector_lo, STEPS)
                nc.vector.tensor_tensor(
                    z0[c % 2], prod[1][:].rearrange("p (t c) -> p t c", c=C),
                    coef[:, Step(c).tiles:Step(c).tiles + TK].unsqueeze(2).broadcast_to([P, TK, C]), ALU.mult,
                ).then_inc(sp_scaled, 1)
                dve.wait_ge(sp_hi, c + 1)
                nc.vector.tensor_tensor(wt_group(1, c), z0[c % 2], wt_group(0, c), ALU.subtract
                                        ).then_inc(sp_lo, 1)

            for s in range(STEPS, TAIL_END):
                if s <= STEPS + SPEC_LAG:
                    first = Step(s)
                    if s < STEPS + 5:
                        first_sweep(first, turning=False)
                    else:
                        add_part(first.back(SPEC_LAG + 1))
                if 0 <= s - SP_TURN - 1 < CHUNKS:
                    split_spectrum(s - SP_TURN - 1)
                if s >= SWEEP2:
                    q = second(s)
                    if q.j >= STEPS + CHUNKS and q.chunk == 2:
                        fold_product(q.back(3))
                    if q.j >= STEPS + CHUNKS and q.chunk == 3:
                        add_rows(q.back(4), q.back(4).block() - 2)
                    low_turned(q, sweep=2)
            with dve.Fori(PAIRS + 1, 2 * PAIRS) as pair:
                q0, b0 = dve.snap(pair * PAIR), dve.snap(pair * 2)
                loads = dve.snap(64 * (pair - PAIRS) + 16 * PAIRS)
                def turn_on_vector(q):
                    c = q.chunk
                    slot, half = q.slot, q.half
                    if half == 0:
                        dve.wait_ge(nat_loaded[slot], loads)
                    buffer, before = raw_use(q.j)
                    dve.wait_ge(*split(b0 + before // CHUNKS, before % CHUNKS))
                    turn_tile(nat[slot][:].rearrange("p t k -> p (t k)").rearrange("p (n f) -> p n f", n=ROWS // Q),
                              half, buffer)

                def low_second(q):
                    dve.wait_ge(at_hi, hi_done(q))
                    c = q.chunk
                    source = turn[BY_PE.index(c)][:] if c in BY_PE else raw_use(q.j)[0]
                    nc.vector.tensor_tensor(at2[c][:, 1], source, at2[c][:, 0], ALU.subtract).then_inc(vector_lo, 1)

                for i in range(2):
                    q = [Step(i * CHUNKS + c, q0, b0) for c in range(CHUNKS)]
                    last = q[0].back(1)
                    turn_on_vector(q[0])
                    turn_on_vector(q[1])
                    turn_on_vector(q[2])
                    turn_on_vector(q[3])
                    turn_on_vector(q[5])
                    low_second(q[3])
                    fold_product(last, sweep=2)
                    turn_on_vector(q[7])
                    low_second(q[4])
                    add_rows(last, dve.snap((last.block() - 2) % BLOCKS))
                    low_second(q[6])
            fold_product(Step(2 * STEPS - 1), sweep=2)
            add_rows(Step(2 * STEPS - 1), BLOCKS - 3)

        @block.tensor
        def _(pe):
            pe.wait_ge(ident_ready, 1)

            def turn_chunk(step, loads, sweep):
                slot, c = step.slot, step.chunk
                if sweep == 2 and loads is None or not step.ran(CHUNKS):
                    bank = c % 2
                else:
                    bank = BY_PE.index(c) if sweep == 2 else BY_PE_1.index(c) % 2
                if loads is not None and step.half == 0:
                    pe.wait_ge(nat_loaded[slot], loads)
                if sweep == 2 and loads is not None:
                    pe.wait_ge(*split(step.back(CHUNKS).block(), step.chunk))
                elif sweep == 2 or isinstance(step.q0, int) and step.j < CHUNKS + 3:
                    if step.ran(2):
                        pe.wait_ge(vector_lo, step.back(2).done())
                else:
                    before = BY_PE_1[BY_PE_1.index(c) - 2]
                    pe.wait_ge(vector_lo, step.back((c - before) % CHUNKS).done())
                order = ordered if sweep == 2 else ordered_1
                for k in range(TK):
                    for n in range(TN):
                        last = nc.tensor.transpose(turn[bank][:, k, n * P:(n + 1) * P],
                                                   order(nat[slot][:, n, :], step.half, k), ident[:])
                last.then_inc(turned, 1)

            def project(step, a=None):
                if a is None:
                    pe.wait_ge(vector_lo, step.done())
                    a = at[step.at_slot]
                bank = prod[step.parity]
                if step.chunk == 0 and step.ran(2 * CHUNKS):
                    pe.wait_ge(x_ready, step.blocks(-1))
                for k in range(TK):
                    n = step.tiles + k
                    nc.tensor.matmul(bank[:], wt[:, 0, n, :], a[:, :, k, :], start=(step.chunk == k == 0), stop=False,
                                     skip_group_check=True)
                    last = nc.tensor.matmul(bank[:, 0:ROWS], wt[:, 1, n, :], a[:, 0, k, :], start=False,
                                            stop=(step.chunk == CHUNKS - 1 and k == TK - 1), skip_group_check=True)
                last.then_inc(projected, 1)

            def spectrum_part(step):
                pe.wait_ge(pool_lo, step.done())
                if step.ran(2):
                    pe.wait_ge(summed, step.back(2).done())
                if step.chunk == 0:
                    pe.wait_ge(h1_lo, step.blocks())
                h, a, bank = h1[step.parity], nsp[step.j % N_NAT], part[step.j % 2]
                for n in range(TN):
                    nc.tensor.matmul(bank[:], h[:, 0, n, :], a[:, 0, n, :], start=(n == 0), stop=False)
                    nc.tensor.matmul(bank[:], h[:, 0, n, :], a[:, 1, n, :], start=False, stop=False)
                    last = nc.tensor.matmul(bank[:], h[:, 1, n, :], a[:, 0, n, :], start=False, stop=(n == TN - 1))
                last.then_inc(spectral, 1)

            def turn_rows(last_step):
                pe.wait_ge(fold_ready, last_step.blocks())
                for n in range(TN):
                    last = nc.tensor.transpose(prod[last_step.parity][:, n * P:(n + 1) * P],
                                               fold[:, n * P:(n + 1) * P], ident[:])
                last.then_inc(rows_turned, 1)

            def first_sweep(step, loads):
                if step.chunk in BY_PE_1 or not step.ran(CHUNKS):
                    turn_chunk(step, loads, 1)
                if step.ran(TURN_LAG):
                    q = step.back(TURN_LAG)
                    if isinstance(step.q0, int) and q.j < CHUNKS:
                        pe.wait_ge(w0_lo, q.j + 1)
                    project(q)
                if step.chunk == 2 and step.ran(CHUNKS):
                    turn_rows(step.back(3))
                if step.ran(SPEC_LAG):
                    spectrum_part(step.back(SPEC_LAG))

            for j in range(PAIR):
                first_sweep(Step(j), 16)
            with pe.Fori(1, PAIRS) as pair:
                q0, b0 = pe.snap(pair * PAIR), pe.snap(pair * 2)
                loads = pe.snap(q0 + 16)
                for j in range(PAIR):
                    first_sweep(Step(j, q0, b0), loads)

            for s in range(STEPS, TAIL_END):
                if s >= SWEEP2:
                    turn_chunk(second(s), None, 2)
                if s < STEPS + TURN_LAG:
                    project(Step(s - TURN_LAG))
                if s >= SWEEP2 + TURN_LAG:
                    q = second(s).back(TURN_LAG)
                    if q.j < STEPS + CHUNKS:
                        pe.wait_ge(sp_lo, q.j - STEPS + 1)
                    project(q)
                if s < STEPS + SPEC_LAG:
                    spectrum_part(Step(s - SPEC_LAG))
                if s == STEPS + 2:
                    turn_rows(Step(s - 3))
                c = s - SP_TURN
                if 0 <= c < CHUNKS:
                    wide = Step(c).wide
                    pe.wait_ge(summed, STEPS - CHUNKS + 2 * wide + 2)
                    if c == 0:
                        pe.wait_ge(x_ready, BLOCKS)
                    else:
                        pe.wait_ge(sp_scaled, c)
                    for k in range(TK):
                        last = nc.tensor.transpose(prod[1][:, k * P:(k + 1) * P],
                                                   ordered(spec[:, wide * WIDE:(wide + 1) * WIDE],
                                                           Step(c).half, k), ident[:])
                    last.then_inc(sp_turned, 1)
                if s >= SWEEP2 and second(s).j == STEPS + CHUNKS + 2:
                    turn_rows(second(s).back(3))
            pe.wait_ge(vector_lo, STEPS + STAYED * CHUNKS)
            for j in range(PAIR - TURN_LAG, PAIR):
                q = Step(STEPS + j)
                project(q, at[q.at_slot][:])
            with pe.Fori(PAIRS + 1, 2 * PAIRS) as pair:
                q0, b0 = pe.snap(pair * PAIR), pe.snap(pair * 2)
                for i in range(2):
                    q = [Step(i * CHUNKS + c, q0, b0) for c in range(CHUNKS)]
                    for c in BY_PE:
                        turn_chunk(q[c], q0, 2)
                    for c in range(CHUNKS):
                        pe.wait_ge(*split(q[c].block(), c))
                        project(q[c], at2[c])
                        if c == 1:
                            turn_rows(q[0].back(1))
            turn_rows(Step(2 * STEPS - 1))


_INS = ['x', 'adj', 'L0_gnn_W', 'L1_gnn_evals', 'L1_gnn_t']
_OUTS = [((4096, 128), 'float32')]


def kernel(**inputs):
    import numpy as _np
    import concourse.bacc as _bacc
    from concourse import mybir as _mybir
    from concourse.bass_utils import run_bass_kernel_spmd as _run

    nc = _bacc.Bacc("TRN2", target_bir_lowering=False, num_devices=1)
    arrays, args = {}, []
    for name in _INS:
        a = _np.ascontiguousarray(inputs[name])
        arrays[f"in_{name}_dram"] = a
        args.append(nc.dram_tensor(f"in_{name}_dram", a.shape, _mybir.dt.from_np(a.dtype), kind="ExternalInput").ap())
    for i, (shape, dtype) in enumerate(_OUTS):
        dt = _mybir.dt.from_np(_np.dtype(dtype))
        args.append(nc.dram_tensor(f"out_{i}_dram", shape, dt, kind="ExternalOutput").ap())
    program(nc, *args)
    r = _run(nc, [arrays], core_ids=[0])
    return r.results[0]["out_0_dram"]
```

```python
from contextlib import ExitStack

import concourse.bass as bass
from concourse import mybir

F32 = mybir.dt.float32
F32R = mybir.dt.float32r
ALU = mybir.AluOpType
ACT = mybir.ActivationFunctionType

P = 128
TN = 2
ROWS = TN * P
TK = 4
COLS = TK * P
EPS = 1e-5
T_MIN = 1e-8
N_AT = 3
N_NAT = 4
TURN_LAG = 2
SPEC_LAG = 13
SPLIT_LAG = 11
Q = 32
WIDE = 2 * COLS
ORDER = ((0, 0), (1, 0), (0, 1), (1, 1), (2, 0), (3, 0), (2, 1), (3, 1))
BY_PE_1 = (0, 2, 4, 6)
BY_VECTOR_1 = (1, 3, 5, 7)
BY_PE = (4, 6)
BY_VECTOR = (0, 1, 2, 3, 5, 7)
LO_VECTOR = (3, 4, 6)
LO_POOL = (0, 1, 2, 5, 7)
HI_ORDER = (0, 1, 2, 3, 4, 5, 7, 6)
ROWS_BY_VECTOR = (3, 5, 7)
ROWS_BY_POOL = (0, 1, 2, 4, 6)


class Step:

    def __init__(self, j, q0=0, b0=0):
        self.j, self.q0, self.b0 = j, q0, b0

    def back(self, n):
        return Step(self.j - n, self.q0, self.b0)

    def ran(self, n):
        return not isinstance(self.q0, int) or self.j >= n

    def done(self):
        return self.q0 + (self.j + 1)

    def block(self):
        return self.b0 + self.j // 8

    def blocks(self, n=1):
        return self.b0 + (self.j // 8 + n)

    @property
    def chunk(self):
        return self.j % 8

    @property
    def parity(self):
        return self.j // 8 % 2

    @property
    def wide(self):
        return ORDER[self.chunk][0]

    @property
    def half(self):
        return ORDER[self.chunk][1]

    @property
    def slot(self):
        return self.parity * 4 + self.wide

    @property
    def tiles(self):
        return (2 * self.wide + self.half) * TK

    @property
    def at_slot(self):
        j = self.j % 16
        return 1 if j == 15 else j % N_AT

    @property
    def before(self):
        return next(n for n in range(1, 16) if self.back(n).at_slot == self.at_slot)


def second_half(wide):
    return ORDER.index((wide, 1))


def program(nc, x, adj, w0, evals, t, out):
    N, C = x.shape
    NT = N // P
    BLOCKS = N // ROWS
    CHUNKS = N // COLS
    STEPS = BLOCKS * CHUNKS
    PAIR = 2 * CHUNKS
    PAIRS = STEPS // PAIR
    assert C == P and CHUNKS == 8 and BLOCKS % 2 == 0
    X_PIECES = 4
    PT = NT // X_PIECES

    with ExitStack() as ctx:
        def sb(name, shape, dt=F32):
            return ctx.enter_context(nc.sbuf_tensor(name, shape, dt))

        def psum(name, shape):
            return ctx.enter_context(nc.psum_tensor(name, shape, F32))

        def sem(name):
            return ctx.enter_context(nc.semaphore(name))

        nat = [sb(f"nat{i}", [P, TN, 2 * COLS]) for i in range(PAIR // 2)]
        at = [sb(f"at{i}", [P, 2, TK, ROWS], F32R) for i in range(N_AT)]
        nsp = [sb(f"nsp{i}", [P, 2, TN, COLS], F32R) for i in range(N_NAT)]
        wt = sb("wt", [P, 2, NT, C], F32R)
        h1_all = sb("h1_all", [P, 2 * TK * ROWS], F32R)
        h1 = [h1_all[:, i * 2 * ROWS:(i + 1) * 2 * ROWS].rearrange("p (h n c) -> p h n c", h=2, n=TN)
              for i in range(2)]
        xs = sb("xs", [P, NT, C])
        spec = sb("spec", [P, N])
        xp = spec[:].rearrange("p (n c) -> p n c", c=C)
        quad = [sb(f"quad{i}", [P, ROWS // Q, TK * Q]) for i in range(2)]
        raw = [spec[:, i * TK * ROWS:(i + 1) * TK * ROWS].rearrange("p (k n) -> p k n", k=TK)
               for i in range(4)]
        h1_turned = h1_all[:].rearrange("p (h k r) -> p h k r", h=2, k=TK)
        nsp_turned = [t_[:].rearrange("p h n (k r) -> p h (n k) r", r=ROWS) for t_ in nsp]
        at2 = nsp_turned + [at[0][:], h1_turned, at[2][:], at[1][:]]
        ident = sb("ident", [P, P])
        half = sb("half", [P, ROWS])
        w_all = half[:, 0:C]
        fold = sb("fold", [P, ROWS])
        z1 = fold[:].rearrange("p (n c) -> p n c", c=C)
        scratch = sb("scratch", [P, 2 * TK * C])
        scaled = [scratch[:, i * TK * C:(i + 1) * TK * C].rearrange("p (k c) -> p k c", c=C)
              for i in range(2)]
        raw1 = scratch[:].rearrange("p (k n) -> p k n", k=TK)
        stats = sb("stats", [P, PT, 6])
        mv0 = sb("mv0", [P, NT, 2])
        mv1 = sb("mv1", [P, TN, 2])
        rstd0 = sb("rstd0", [P, NT])
        shift0 = sb("shift0", [P, NT])
        rstd1 = sb("rstd1", [P, TN])
        lnv = sb("lnv", [P, 6, PT])
        tneg = sb("tneg", [P, 1])
        coef = sb("coef", [P, NT])

        turn = [psum(f"turn{i}", [P, TK, ROWS]) for i in range(2)]
        prod = [psum(f"prod{i}", [P, 2 * ROWS]) for i in range(2)]
        part = [psum(f"part{i}", [P, COLS]) for i in range(2)]

        x_loaded = [sem(f"x_loaded{i}") for i in range(X_PIECES)]
        w_loaded, t_loaded, ev_loaded = sem("w_loaded"), sem("t_loaded"), sem("ev_loaded")
        xs_loaded = sem("xs_loaded")
        quad_loaded = [sem(f"quad_loaded{i}") for i in range(2)]
        nat_loaded = [sem(f"nat_loaded{i}") for i in range(PAIR // 2)]
        stored = sem("stored")
        zeroed, ident_ready = sem("zeroed"), sem("ident_ready")
        spec_zeroed = sem("spec_zeroed")
        t_ready, coef_ready = sem("t_ready"), sem("coef_ready")
        raw_turned = sem("raw_turned")
        turned, at_hi, vector_lo, projected = sem("turned"), sem("at_hi"), sem("vector_lo"), sem("projected")
        nat_hi, pool_lo, spectral, summed = sem("nat_hi"), sem("pool_lo"), sem("spectral"), sem("summed")
        vector_nat = sem("vector_nat")
        half_ready, fold_ready, rows_turned = sem("half_ready"), sem("fold_ready"), sem("rows_turned")
        x_ready, z1_ready = sem("x_ready"), sem("z1_ready")
        h1_hi, h1_lo = sem("h1_hi"), sem("h1_lo")
        ln_stats, ln_moments, ln_var, ln_sqrt = sem("ln_stats"), sem("ln_moments"), sem("ln_var"), sem("ln_sqrt")
        ln_recip, ln_square, ln_resid, ln_factor = sem("ln_recip"), sem("ln_square"), sem("ln_resid"), sem("ln_factor")
        ln_rstd, ln_shift = sem("ln_rstd"), sem("ln_shift")
        z0_ready, w0_ready, w0_hi, w0_lo = sem("z0_ready"), sem("w0_ready"), sem("w0_hi"), sem("w0_lo")
        w0_normed, w0_vector = sem("w0_normed"), sem("w0_vector")
        sp_turned, sp_scaled, sp_hi, sp_lo = sem("sp_turned"), sem("sp_scaled"), sem("sp_hi"), sem("sp_lo")

        adj_v = adj.rearrange("(b t p) k -> b p t k", t=TN, p=P)
        out_v = out.rearrange("(b t p) c -> b p t c", t=TN, p=P)
        adj_q = adj.rearrange("(b n r) (m g f) -> b m g r n f", n=ROWS // Q, r=Q, g=P // Q, f=WIDE // 4)
        x_v = x.rearrange("(t p) c -> p t c", p=P)
        adj_c = adj.rearrange("(b n r) (m g f) -> b m g r n f", n=ROWS // Q, r=Q, g=P // Q, f=COLS // 4)
        x_wide = x.rearrange("(m h p j) c -> m p h (j c)", h=2, p=P, j=TK)
        SP_TURN = STEPS + SPEC_LAG + 3 - CHUNKS
        SWEEP2 = SP_TURN
        TAIL_END = SWEEP2 + PAIR

        def second(s):
            return Step(STEPS + s - SWEEP2)

        def wt_group(part, c):
            n = Step(c).tiles
            return wt[:, part, n:n + TK, :]

        def ordered(columns, half, k):
            return columns.rearrange("p (q j) -> p j q", q=P)[:, half * TK + k]

        def ordered_1(columns, half, k):
            return columns[:, half * COLS:(half + 1) * COLS].rearrange("p (q j) -> p j q", q=P)[:, k]

        def turned_by_pe_1(b, c):
            return b * len(BY_PE_1) + (CHUNKS - len(BY_PE_1) + BY_PE_1.index(c) + 1)

        def turned_by_vector_1(b, c):
            return b * len(BY_VECTOR_1) + (BY_VECTOR_1.index(c) + 1 - len(BY_VECTOR_1))

        TURNED_1 = turned_by_pe_1(BLOCKS - 1, BY_PE_1[-1])
        RAW_1 = turned_by_vector_1(BLOCKS - 1, BY_VECTOR_1[-1])

        NAT_BY_VECTOR = [STEPS - SPLIT_LAG + i for i in (1, 5, 7, 9)]

        def nat_split(step):
            if not isinstance(step.q0, int):
                return pool_lo, step.done()
            earlier = sum(j < step.j for j in NAT_BY_VECTOR)
            if step.j in NAT_BY_VECTOR:
                return vector_nat, earlier + 1
            return pool_lo, step.done() - earlier

        STAYED = 2

        def turned_stayed(q):
            return TURNED_1 + q.j - STEPS + 1

        def turned_by_pe(b, c):
            return (b - (BLOCKS + STAYED)) * len(BY_PE) + (TURNED_1 + STAYED * CHUNKS + BY_PE.index(c) + 1)

        def turned_by_vector(b, c):
            return (b - (BLOCKS + STAYED)) * len(BY_VECTOR) + (RAW_1 + BY_VECTOR.index(c) + 1)

        def split(b, c):
            if c in LO_VECTOR:
                return vector_lo, ((b - (BLOCKS + STAYED)) * len(LO_VECTOR)
                                   + (STEPS + STAYED * CHUNKS + LO_VECTOR.index(c) + 1))
            return pool_lo, ((b - (BLOCKS + STAYED)) * len(LO_POOL)
                             + (STEPS - len(NAT_BY_VECTOR) + LO_POOL.index(c) + 1))

        def hi_done(q):
            return q.q0 + (q.j - q.chunk + HI_ORDER.index(q.chunk) + 1)

        def raw_use(j):
            uses = [8 * i + c for i in range(-2, 2) for c in BY_VECTOR]
            n = uses.index(j)
            return raw[(n - 2 * len(BY_VECTOR)) % 4], uses[n - 4]

        block = ctx.enter_context(nc.Block())

        @block.sync
        def _(sp):
            def load(slot, source_block, m):
                sp.dma_start(nat[slot][:], adj_v[source_block, :, :, m * WIDE:(m + 1) * WIDE]
                             ).then_inc(nat_loaded[slot], 16)

            def load_quad(tile, source_block, m, loaded):
                for g in range(P // Q):
                    sp.dma_start(tile[g * Q:(g + 1) * Q], adj_q[source_block, m, g]).then_inc(loaded, 16)

            def load_x(i):
                sp.dma_start(spec[:, i * PT * C:(i + 1) * PT * C].rearrange("p (h f) -> p h f", h=2), x_wide[i]
                             ).then_inc(x_loaded[i], 16)

            def load_again(source_block, c):
                n, chunk = c // 2 % 2, Step(c)
                for g in range(P // Q):
                    sp.dma_start(quad[n][g * Q:(g + 1) * Q], adj_c[source_block, 2 * chunk.wide + chunk.half, g]
                                 ).then_inc(quad_loaded[n], 16)

            load_x(0)
            load_x(1)
            load(0, 0, 0)
            load_x(2)
            load(1, 0, 1)
            load_x(3)
            load(2, 0, 2)
            load(3, 0, 3)
            load(4, 1, 0)
            sp.dma_start(xs[:], x_v).then_inc(xs_loaded, 16)
            load(5, 1, 1)
            load_again(1, 1)
            load(6, 1, 2)
            load_again(1, 3)
            load(7, 1, 3)
            for c in (5, 7):
                sp.wait_ge(raw_turned, turned_by_vector_1(1, c - 4))
                load_again(1, c)
            with sp.Fori(1, PAIRS) as pair:
                q0, b0 = sp.snap(pair * PAIR), sp.snap(pair * 2)
                quad_free = [{c: sp.snap(turned_by_vector_1(b0 + (i + c // 4 - 1), (c + 4) % CHUNKS))
                              for c in BY_VECTOR_1} for i in range(2)]
                for i in range(2):
                    def load_own(m):
                        sp.wait_ge(pool_lo, Step(i * CHUNKS + 2 * m + 1, q0, b0).back(PAIR).done())
                        load(i * 4 + m, b0 + i, m)

                    for c in BY_VECTOR_1:
                        load_own(c // 2)
                        sp.wait_ge(raw_turned, quad_free[i][c])
                        load_again(b0 + i, c)

            def load_second(b, m, parity, source_block):
                slot = parity * 4 + m
                if second_half(m) in BY_PE:
                    load(slot, source_block, m)
                else:
                    tile = nat[slot][:].rearrange("p t k -> p (t k)").rearrange("p (n f) -> p n f", n=ROWS // Q)
                    load_quad(tile, source_block, m, nat_loaded[slot])

            def store(b, place):
                sp.wait_ge(x_ready, b + 1)
                rows = xs[:, place * TN:(place + 1) * TN, :] if isinstance(place, int) else \
                    xs[:, bass.ds(place * TN, TN), :]
                sp.dma_start(out_v[place], rows).then_inc(stored, 16)

            for b in range(BLOCKS + STAYED, BLOCKS + 2 * STAYED):
                for m in range(4):
                    sp.wait_ge(turned, turned_stayed(Step((b - STAYED) * CHUNKS + second_half(m))))
                    load_second(b, m, b % 2, b - (BLOCKS + STAYED))
            store(BLOCKS, BLOCKS - 2)
            with sp.Fori(PAIRS + 2, 2 * PAIRS) as pair:
                b0 = sp.snap(pair * 2)
                source = sp.snap(b0 - (BLOCKS + 2))
                places = [sp.snap((b0 + (i - 5)) % BLOCKS) for i in range(2)]
                for i in range(2):
                    for m in range(4):
                        c = second_half(m)
                        if c in BY_PE:
                            sp.wait_ge(turned, turned_by_pe(b0 + (i - 2), c))
                        else:
                            sp.wait_ge(raw_turned, turned_by_vector(b0 + (i - 2), c))
                        load_second(b0 + i, m, i, source + i)
                    store(b0 + (i - 3), places[i])
            for b in range(2 * BLOCKS - 3, 2 * BLOCKS):
                store(b, b - (BLOCKS + STAYED))
            sp.wait_ge(stored, 16 * BLOCKS)

        @block.gpsimd
        def _(pool):
            nc.gpsimd.memset(ident[:], 0.0).then_inc(zeroed, 1)
            pool.wait_ge(zeroed, 1)
            nc.gpsimd.affine_select(out=ident[:], in_=ident[:], compare_op=ALU.not_equal, fill=1.0, base=0,
                                    pattern=[[-1, P]], channel_multiplier=1).then_inc(ident_ready, 1)

            def hidden_rows(g):
                pool.wait_ge(z0_ready, ROWS_BY_POOL.index(g) + 1)
                if g == 0:
                    pool.wait_ge(w_loaded, 16)
                n = Step(g).tiles
                nc.gpsimd.tensor_tensor(xp[:, n:n + TK, :], xp[:, n:n + TK, :],
                                        w_all.unsqueeze(1).broadcast_to([P, TK, C]), ALU.mult).then_inc(w0_ready, 1)

            def low_rows(g):
                pool.wait_ge(w0_hi, g + 1)
                n = Step(g).tiles
                nc.gpsimd.tensor_tensor(wt_group(1, g), xp[:, n:n + TK, :], wt_group(0, g), ALU.subtract
                                        ).then_inc(w0_lo, 1)

            def low_nat(step):
                pool.wait_ge(nat_hi, step.done())
                slot, c = step.j % PAIR // 2, step.j % 2
                nc.gpsimd.tensor_tensor(nsp[step.j % N_NAT][:, 1], nat[slot][:, :, c * COLS:(c + 1) * COLS],
                                        nsp[step.j % N_NAT][:, 0], ALU.subtract).then_inc(pool_lo, 1)

            hidden_rows(0)
            for j in range(PAIR):
                if j + 1 in ROWS_BY_POOL:
                    hidden_rows(j + 1)
                if j < CHUNKS:
                    low_rows(j)
                if j == CHUNKS:
                    pool.wait_ge(w0_lo, CHUNKS)
                    nc.gpsimd.memset(spec[:], 0.0).then_inc(spec_zeroed, 1)
                if j >= SPLIT_LAG:
                    low_nat(Step(j - SPLIT_LAG))
            with pool.Fori(1, PAIRS) as pair:
                q0 = pool.snap(pair * PAIR)
                for j in range(PAIR):
                    low_nat(Step(j, q0).back(SPLIT_LAG))
            for s in range(STEPS, SP_TURN + 1 + CHUNKS):
                if s < STEPS + SPLIT_LAG and s - SPLIT_LAG not in NAT_BY_VECTOR:
                    low_nat(Step(s - SPLIT_LAG))
                c = s - SP_TURN - 1
                if c >= 0:
                    pool.wait_ge(sp_hi, c + 1)
                    nc.gpsimd.tensor_tensor(wt_group(1, c), scaled[c % 2], wt_group(0, c), ALU.subtract
                                            ).then_inc(sp_lo, 1)

            with pool.Fori(PAIRS + 1, 2 * PAIRS) as pair:
                q0, b0 = pool.snap(pair * PAIR), pool.snap(pair * 2)
                for i in range(2):
                    for c in LO_POOL:
                        q = Step(i * CHUNKS + c, q0, b0)
                        pool.wait_ge(at_hi, hi_done(q))
                        nc.gpsimd.tensor_tensor(at2[c][:, 1], raw_use(q.j)[0], at2[c][:, 0], ALU.subtract
                                                ).then_inc(pool_lo, 1)

        @block.scalar
        def _(act):
            act.dma_start(tneg[:], t.rearrange("(a b) -> a b", a=1).partition_broadcast(P)
                          ).then_inc(t_loaded, 16)
            act.dma_start(coef[:].rearrange("p (m j) -> p m j", j=WIDE // P),
                          evals.rearrange("(m p j) -> p m j", p=P, j=WIDE // P)).then_inc(ev_loaded, 16)
            act.dma_start(w_all, w0.rearrange("(a b) -> a b", a=1).partition_broadcast(P)
                          ).then_inc(w_loaded, 16)

            def root(n, tiles):
                act.wait_ge(ln_var, n)
                nc.scalar.activation(lnv[:, 1, 0:tiles], lnv[:, 0, 0:tiles], ACT.Sqrt).then_inc(ln_sqrt, 1)

            def relu_rows(g):
                if Step(g).half == 0:
                    act.wait_ge(ln_shift, Step(g).wide + 1)
                for i in range(TK):
                    n = Step(g).tiles + i
                    last = nc.scalar.activation(xp[:, n, :], xp[:, n, :], ACT.Relu,
                                                bias=shift0[:, n:n + 1], scale=rstd0[:, n:n + 1])
                last.then_inc(z0_ready, 1)

            def high_rows(g):
                if g in ROWS_BY_VECTOR:
                    act.wait_ge(w0_vector, ROWS_BY_VECTOR.index(g) + 1)
                else:
                    act.wait_ge(w0_ready, ROWS_BY_POOL.index(g) + 1)
                n = Step(g).tiles
                nc.scalar.activation(wt_group(0, g), xp[:, n:n + TK, :], ACT.Copy).then_inc(w0_hi, 1)

            def high_turned(step, sweep=1):
                c = step.chunk
                source = turn[c % 2][:]
                if sweep == 2:
                    act.wait_ge(turned, turned_stayed(step))
                elif isinstance(step.q0, int) and step.j < CHUNKS:
                    act.wait_ge(turned, step.done())
                elif c in BY_PE_1:
                    act.wait_ge(turned, turned_by_pe_1(step.block(), c))
                    source = turn[BY_PE_1.index(c) % 2][:]
                else:
                    act.wait_ge(raw_turned, turned_by_vector_1(step.block(), c))
                    source = raw1
                if step.ran(step.before):
                    act.wait_ge(projected, step.back(step.before).done())
                nc.scalar.activation(at[step.at_slot][:, 0], source, ACT.Copy).then_inc(at_hi, 1)

            def high_nat(step):
                slot, c = step.j % PAIR // 2, step.j % 2
                if c == 0:
                    act.wait_ge(nat_loaded[slot], step.q0 + (step.j // PAIR + 1) * 16)
                if step.ran(N_NAT):
                    act.wait_ge(spectral, step.back(N_NAT).done())
                nc.scalar.activation(nsp[step.j % N_NAT][:, 0], nat[slot][:, :, c * COLS:(c + 1) * COLS],
                                     ACT.Copy).then_inc(nat_hi, 1)

            def copy_half(last):
                act.wait_ge(projected, last.done())
                if last.ran(CHUNKS):
                    act.wait_ge(fold_ready, last.blocks(0))
                nc.scalar.activation(half[:], prod[last.parity][:, ROWS:2 * ROWS], ACT.Copy
                                     ).then_inc(half_ready, 1)

            def high_h1(last):
                act.wait_ge(z1_ready, last.blocks())
                nc.scalar.activation(h1[last.parity][:, 0], z1, ACT.Relu).then_inc(h1_hi, 1)

            def first_sweep(step):
                if step.chunk == 2 and step.ran(CHUNKS):
                    copy_half(step.back(3))
                ends = step.ran(CHUNKS)
                if step.ran(SPLIT_LAG):
                    high_nat(step.back(SPLIT_LAG))
                if step.chunk == 4 and ends:
                    root(step.back(5).blocks(X_PIECES + 1), TN)
                high_turned(step)
                if step.chunk == 4 and ends:
                    high_h1(step.back(5))

            root(1, PT)
            relu_rows(0)
            root(2, PT)
            for j in range(PAIR):
                if j == 0:
                    high_rows(j)
                if j + 1 in ROWS_BY_POOL:
                    relu_rows(j + 1)
                if j == 3:
                    root(4, PT)
                if 0 < j < CHUNKS:
                    high_rows(j)
                first_sweep(Step(j))
                if j == 0:
                    root(3, PT)
            with act.Fori(1, PAIRS) as pair:
                q0, b0 = act.snap(pair * PAIR), act.snap(pair * 2)
                for j in range(PAIR):
                    first_sweep(Step(j, q0, b0))

            def high_spectrum(c):
                act.wait_ge(sp_scaled, c + 1)
                nc.scalar.activation(wt_group(0, c), scaled[c % 2], ACT.Copy).then_inc(sp_hi, 1)

            for s in range(STEPS, TAIL_END):
                if s < STEPS + SPLIT_LAG:
                    if s == STEPS + 2:
                        copy_half(Step(s).back(3))
                    high_nat(Step(s - SPLIT_LAG))
                    if s == STEPS + 4:
                        root(Step(s).back(5).blocks(X_PIECES + 1), TN)
                        high_h1(Step(s).back(5))
                if s == STEPS + 5:
                    act.wait_ge(t_ready, 1)
                    act.wait_ge(ev_loaded, 16)
                    nc.scalar.activation(coef[:], coef[:], ACT.Exp, scale=tneg[:, 0:1]).then_inc(coef_ready, 1)
                if 0 <= s - SP_TURN - 1 < CHUNKS:
                    high_spectrum(s - SP_TURN - 1)
                if s >= SWEEP2:
                    q = second(s)
                    if q.chunk == 2 and q.j >= STEPS + CHUNKS:
                        copy_half(q.back(3))
                    high_turned(q, sweep=2)
            with act.Fori(PAIRS + 1, 2 * PAIRS) as pair:
                q0, b0 = act.snap(pair * PAIR), act.snap(pair * 2)
                for j in [i * CHUNKS + c for i in range(2) for c in HI_ORDER]:
                    q = Step(j, q0, b0)
                    c = q.chunk
                    act.wait_ge(projected, q.back(CHUNKS).done())
                    if c in BY_PE:
                        act.wait_ge(turned, turned_by_pe(q.block(), c))
                        source = turn[BY_PE.index(c)][:]
                    else:
                        act.wait_ge(raw_turned, turned_by_vector(q.block(), c))
                        source = raw_use(j)[0]
                    nc.scalar.activation(at2[c][:, 0], source, ACT.Copy).then_inc(at_hi, 1)
                    if c == 3:
                        copy_half(q.back(4))
            copy_half(Step(2 * STEPS - 1))

        @block.vector
        def _(dve):
            dve.wait_ge(t_loaded, 16)
            nc.vector.tensor_scalar(tneg[:], tneg[:], T_MIN, -1.0, ALU.max, ALU.mult).then_inc(t_ready, 1)

            def row_stats(rows, tiles):
                for i in range(tiles):
                    last = nc.vector.bn_stats(stats[:, i, :], rows[:, i, :])
                last.then_inc(ln_stats, 1)

            def moments(n, mv, tiles):
                for i in range(tiles):
                    last = nc.vector.bn_aggr(mv[:, i, :], stats[:, i, :])
                last.then_inc(ln_moments, 1)
                dve.wait_ge(ln_moments, n)
                nc.vector.tensor_scalar(lnv[:, 0, 0:tiles], mv[:, :, 1], EPS, None, ALU.add).then_inc(ln_var, 1)

            def inverse_root(n, rstd, tiles):
                v, root, r, rr, vrr, f = (lnv[:, i, 0:tiles] for i in range(6))
                dve.wait_ge(ln_sqrt, n)
                nc.vector.reciprocal(r, root).then_inc(ln_recip, 1)
                dve.wait_ge(ln_recip, n)
                nc.vector.tensor_tensor(rr, r, r, ALU.mult).then_inc(ln_square, 1)
                dve.wait_ge(ln_square, n)
                nc.vector.tensor_tensor(vrr, rr, v, ALU.mult).then_inc(ln_resid, 1)
                dve.wait_ge(ln_resid, n)
                nc.vector.tensor_scalar(f, vrr, -0.5, 1.5, ALU.mult, ALU.add).then_inc(ln_factor, 1)
                dve.wait_ge(ln_factor, n)
                nc.vector.tensor_tensor(rstd, r, f, ALU.mult).then_inc(ln_rstd, 1)
                dve.wait_ge(ln_rstd, n)

            def x_moments(i):
                dve.wait_ge(x_loaded[i], 16)
                row_stats(xp[:, i * PT:(i + 1) * PT, :], PT)
                dve.wait_ge(ln_stats, i + 1)
                moments(i + 1, mv0[:, i * PT:(i + 1) * PT, :], PT)

            def x_rstd(i):
                piece = slice(i * PT, (i + 1) * PT)
                inverse_root(i + 1, rstd0[:, piece], PT)
                nc.vector.scalar_tensor_tensor(out=shift0[:, piece], in0=mv0[:, piece, 0], scalar=-1.0,
                                               in1=rstd0[:, piece], op0=ALU.mult, op1=ALU.mult).then_inc(ln_shift, 1)

            def vector_rows(g):
                if g == ROWS_BY_VECTOR[0]:
                    dve.wait_ge(w_loaded, 16)
                dve.wait_ge(ln_shift, Step(g).wide + 1)
                n = Step(g).tiles
                for i in range(n, n + TK):
                    last = nc.vector.tensor_scalar(xp[:, i, :], xp[:, i, :], rstd0[:, i:i + 1], shift0[:, i:i + 1],
                                                   ALU.mult, ALU.add)
                last.then_inc(w0_normed, 1)
                dve.wait_ge(w0_normed, ROWS_BY_VECTOR.index(g) + 1)
                nc.vector.scalar_tensor_tensor(
                    out=xp[:, n:n + TK, :], in0=xp[:, n:n + TK, :], scalar=0.0,
                    in1=w_all.unsqueeze(1).broadcast_to([P, TK, C]), op0=ALU.max, op1=ALU.mult,
                ).then_inc(w0_vector, 1)

            def by_vector_1(step):
                return step.chunk in BY_VECTOR_1 and step.ran(CHUNKS)

            def low_turned(step, sweep=1):
                dve.wait_ge(at_hi, step.done())
                if sweep == 2 or not step.ran(CHUNKS):
                    source = turn[step.chunk % 2][:]
                else:
                    source = raw1 if by_vector_1(step) else turn[BY_PE_1.index(step.chunk) % 2][:]
                nc.vector.tensor_tensor(at[step.at_slot][:, 1], source, at[step.at_slot][:, 0],
                                        ALU.subtract).then_inc(vector_lo, 1)

            def turn_tile(tile, half, buffer):
                chunk = tile.rearrange("p n (i j) -> p j n i", i=Q)[:, half * TK:(half + 1) * TK]
                nc.vector.transpose(buffer.rearrange("p k (n r) -> p k n r", r=Q), chunk).then_inc(raw_turned, 1)

            def turn_on_vector_1(step):
                c = step.chunk
                n = c // 2 % 2
                dve.wait_ge(quad_loaded[n], step.block() * 128 + (c // 4 - 1) * 64)
                dve.wait_ge(vector_lo, step.back(2).done())
                turn_tile(quad[n][:], 0, raw1)

            def add_part(step, halves=(0, 1)):
                if 0 in halves:
                    dve.wait_ge(spectral, step.done())
                    if step.ran(1):
                        dve.wait_ge(summed, step.back(1).done())
                columns = slice(halves[0] * COLS // 2, (halves[-1] + 1) * COLS // 2)
                cols = spec[:, step.chunk * COLS:(step.chunk + 1) * COLS][:, columns]
                last = nc.vector.tensor_tensor(cols, part[step.j % 2][:, columns], cols, ALU.add)
                if 1 in halves:
                    last.then_inc(summed, 1)

            def low_nat(step):
                dve.wait_ge(nat_hi, step.done())
                slot, c = step.j % PAIR // 2, step.j % 2
                nc.vector.tensor_tensor(nsp[step.j % N_NAT][:, 1], nat[slot][:, :, c * COLS:(c + 1) * COLS],
                                        nsp[step.j % N_NAT][:, 0], ALU.subtract).then_inc(vector_nat, 1)

            def fold_product(last, sweep=1):
                if sweep == 1 and last.ran(CHUNKS):
                    dve.wait_ge(h1_lo, last.blocks(0))
                dve.wait_ge(half_ready, last.blocks())
                nc.vector.tensor_tensor(fold[:], prod[last.parity][:, 0:ROWS], half[:], ALU.add
                                        ).then_inc(fold_ready, 1)

            def block_rows(row):
                return xs[:, row * TN:(row + 1) * TN, :] if isinstance(row, int) else xs[:, bass.ds(row * TN, TN), :]

            def add_rows(last, row):
                dve.wait_ge(rows_turned, last.blocks())
                rows = block_rows(row)
                nc.vector.tensor_tensor(rows, prod[last.parity][:, 0:ROWS].rearrange("p (t c) -> p t c", c=C),
                                        rows, ALU.add).then_inc(x_ready, 1)
                return rows

            def norm_block(rows):
                for i in range(TN):
                    last = nc.vector.tensor_scalar(z1[:, i, :], rows[:, i, :], mv1[:, i, 0:1], rstd1[:, i:i + 1],
                                                   ALU.subtract, ALU.mult)
                last.then_inc(z1_ready, 1)

            def low_h1(last):
                dve.wait_ge(h1_hi, last.blocks())
                nc.vector.scalar_tensor_tensor(out=h1[last.parity][:, 1], in0=z1, scalar=0.0,
                                               in1=h1[last.parity][:, 0], op0=ALU.max, op1=ALU.subtract
                                               ).then_inc(h1_lo, 1)

            def first_sweep(step):
                ends = step.ran(CHUNKS)

                def turn_next():
                    if by_vector_1(step.back(-1)):
                        turn_on_vector_1(step.back(-1))

                def add(halves=(0, 1)):
                    if step.ran(SPEC_LAG + 1):
                        add_part(step.back(SPEC_LAG + 1), halves)

                if not ends or step.chunk not in (3, 4):
                    add()
                if step.chunk == 3 and ends:
                    last = step.back(4)
                    n = last.blocks(X_PIECES + 1)
                    if isinstance(step.q0, int) and step.j < PAIR:
                        dve.wait_ge(xs_loaded, 16)
                    rows = add_rows(last, last.block())
                    dve.wait_ge(x_ready, last.blocks())
                    add(halves=(0,))
                    row_stats(rows, TN)
                    dve.wait_ge(ln_stats, n)
                    add(halves=(1,))
                    moments(n, mv1[:], TN)
                    low_turned(step)
                elif step.chunk == 4 and ends:
                    last = step.back(5)
                    inverse_root(last.blocks(X_PIECES + 1), rstd1[:], TN)
                    norm_block(block_rows(last.block()))
                    add()
                    low_h1(last)
                    low_turned(step)
                    turn_next()
                else:
                    if step.chunk == 2 and ends:
                        fold_product(step.back(3))
                    low_turned(step)
                    turn_next()

            def last_block(step):
                last = Step(STEPS - 1)
                n = last.blocks(X_PIECES + 1)
                if step.chunk == 2:
                    fold_product(last)
                if step.chunk == 3:
                    rows = add_rows(last, last.block())
                    dve.wait_ge(x_ready, last.blocks())
                    row_stats(rows, TN)
                    dve.wait_ge(ln_stats, n)
                    moments(n, mv1[:], TN)
                if step.chunk == 4:
                    inverse_root(n, rstd1[:], TN)
                    norm_block(block_rows(last.block()))
                add_part(step.back(SPEC_LAG + 1))
                if step.chunk == 4:
                    low_h1(last)

            x_moments(0)
            x_rstd(0)
            x_moments(1)
            x_rstd(1)
            x_moments(2)
            for j in range(PAIR):
                if j == SPEC_LAG + 1:
                    dve.wait_ge(spec_zeroed, 1)
                first_sweep(Step(j))
                if j == 0:
                    x_rstd(2)
                    vector_rows(3)
                if j == 1:
                    x_moments(3)
                if j == 2:
                    x_rstd(3)
                if j in (3, 5):
                    vector_rows(j + 2)
            with dve.Fori(1, PAIRS) as pair:
                q0, b0 = dve.snap(pair * PAIR), dve.snap(pair * 2)
                for j in range(PAIR):
                    first_sweep(Step(j, q0, b0))

            def scale_spectrum(c):
                dve.wait_ge(sp_turned, c + 1)
                if c >= 2:
                    dve.wait_ge(sp_lo, c - 1)
                if c == 0:
                    dve.wait_ge(coef_ready, 1)
                    dve.wait_ge(vector_lo, STEPS)
                nc.vector.tensor_tensor(
                    scaled[c % 2], prod[1][:].rearrange("p (t c) -> p t c", c=C),
                    coef[:, Step(c).tiles:Step(c).tiles + TK].unsqueeze(2).broadcast_to([P, TK, C]), ALU.mult,
                ).then_inc(sp_scaled, 1)

            AHEAD = 3
            FIRST_LOADS = 64 + 16 * PAIRS

            def turn_on_vector(q, loads, fresh=False):
                slot, half = q.slot, q.half
                if half == 0:
                    dve.wait_ge(nat_loaded[slot], loads)
                buffer, before = raw_use(q.j)
                if not fresh:
                    dve.wait_ge(*split(q.b0 + before // CHUNKS, before % CHUNKS))
                turn_tile(nat[slot][:].rearrange("p t k -> p (t k)").rearrange("p (n f) -> p n f", n=ROWS // Q),
                          half, buffer)

            def low_second(q):
                dve.wait_ge(at_hi, hi_done(q))
                c = q.chunk
                source = turn[BY_PE.index(c)][:] if c in BY_PE else raw_use(q.j)[0]
                nc.vector.tensor_tensor(at2[c][:, 1], source, at2[c][:, 0], ALU.subtract).then_inc(vector_lo, 1)

            for s in range(STEPS, TAIL_END):
                if 0 <= s - SP_TURN - 1 < CHUNKS:
                    scale_spectrum(s - SP_TURN - 1)
                if s <= STEPS + SPEC_LAG:
                    first = Step(s)
                    if s < STEPS + 5:
                        last_block(first)
                    else:
                        add_part(first.back(SPEC_LAG + 1))
                    if s - SPLIT_LAG in NAT_BY_VECTOR:
                        low_nat(Step(s - SPLIT_LAG))
                if s >= SWEEP2:
                    q = second(s)
                    if q.j >= STEPS + CHUNKS and q.chunk == 2:
                        fold_product(q.back(3))
                    if q.j >= STEPS + CHUNKS and q.chunk == 3:
                        add_rows(q.back(4), q.back(4).block() - 2)
                    low_turned(q, sweep=2)
                    c = s - (TAIL_END - 6)
                    if 0 <= c < AHEAD:
                        turn_on_vector(Step(c, STEPS + PAIR, BLOCKS + STAYED), FIRST_LOADS, fresh=True)
            def second_blocks(q0, b0, loads, final):
                for i in range(2):
                    q = [Step(i * CHUNKS + c, q0, b0) for c in range(CHUNKS)]
                    last = q[0].back(1)
                    turn_on_vector(q[3], loads)
                    turn_on_vector(q[5], loads)
                    low_second(q[3])
                    fold_product(last, sweep=2)
                    turn_on_vector(q[7], loads)
                    low_second(q[4])
                    place = (last.block() - 2) % BLOCKS
                    add_rows(last, place if final else dve.snap(place))
                    low_second(q[6])
                    for c in range(AHEAD):
                        if i == 0:
                            turn_on_vector(Step(CHUNKS + c, q0, b0), loads)
                        elif not final:
                            turn_on_vector(Step(c, dve.snap(q0 + PAIR), dve.snap(b0 + 2)), dve.snap(loads + 64))

            with dve.Fori(PAIRS + 1, 2 * PAIRS - 1) as pair:
                second_blocks(dve.snap(pair * PAIR), dve.snap(pair * 2),
                              dve.snap(64 * (pair - PAIRS) + 16 * PAIRS), final=False)
            second_blocks((2 * PAIRS - 1) * PAIR, (2 * PAIRS - 1) * 2, FIRST_LOADS + 64 * (PAIRS - 2), final=True)
            fold_product(Step(2 * STEPS - 1), sweep=2)
            add_rows(Step(2 * STEPS - 1), BLOCKS - 3)

        @block.tensor
        def _(pe):
            pe.wait_ge(ident_ready, 1)

            def turn_chunk(step, loads, sweep):
                slot, c = step.slot, step.chunk
                if sweep == 2 and loads is None or not step.ran(CHUNKS):
                    bank = c % 2
                else:
                    bank = BY_PE.index(c) if sweep == 2 else BY_PE_1.index(c) % 2
                if loads is not None and step.half == 0:
                    pe.wait_ge(nat_loaded[slot], loads)
                if sweep == 2 and loads is not None:
                    pe.wait_ge(*split(step.back(CHUNKS).block(), step.chunk))
                elif sweep == 2 or isinstance(step.q0, int) and step.j < CHUNKS + 3:
                    if step.ran(2):
                        pe.wait_ge(vector_lo, step.back(2).done())
                else:
                    before = BY_PE_1[BY_PE_1.index(c) - 2]
                    pe.wait_ge(vector_lo, step.back((c - before) % CHUNKS).done())
                order = ordered if sweep == 2 else ordered_1
                for k in range(TK):
                    for n in range(TN):
                        last = nc.tensor.transpose(turn[bank][:, k, n * P:(n + 1) * P],
                                                   order(nat[slot][:, n, :], step.half, k), ident[:])
                last.then_inc(turned, 1)

            def project(step, a=None):
                if a is None:
                    pe.wait_ge(vector_lo, step.done())
                    a = at[step.at_slot]
                bank = prod[step.parity]
                if step.chunk == 0 and step.ran(2 * CHUNKS):
                    pe.wait_ge(x_ready, step.blocks(-1))
                for k in range(TK):
                    n = step.tiles + k
                    nc.tensor.matmul(bank[:], wt[:, 0, n, :], a[:, :, k, :], start=(step.chunk == k == 0), stop=False,
                                     skip_group_check=True)
                    last = nc.tensor.matmul(bank[:, 0:ROWS], wt[:, 1, n, :], a[:, 0, k, :], start=False,
                                            stop=(step.chunk == CHUNKS - 1 and k == TK - 1), skip_group_check=True)
                last.then_inc(projected, 1)

            def spectrum_part(step):
                pe.wait_ge(*nat_split(step))
                if step.ran(2):
                    pe.wait_ge(summed, step.back(2).done())
                if step.chunk == 0:
                    pe.wait_ge(h1_lo, step.blocks())
                h, a, bank = h1[step.parity], nsp[step.j % N_NAT], part[step.j % 2]
                for n in range(TN):
                    nc.tensor.matmul(bank[:], h[:, 0, n, :], a[:, 0, n, :], start=(n == 0), stop=False)
                    nc.tensor.matmul(bank[:], h[:, 0, n, :], a[:, 1, n, :], start=False, stop=False)
                    last = nc.tensor.matmul(bank[:], h[:, 1, n, :], a[:, 0, n, :], start=False, stop=(n == TN - 1))
                last.then_inc(spectral, 1)

            def turn_rows(last_step):
                pe.wait_ge(fold_ready, last_step.blocks())
                for n in range(TN):
                    last = nc.tensor.transpose(prod[last_step.parity][:, n * P:(n + 1) * P],
                                               fold[:, n * P:(n + 1) * P], ident[:])
                last.then_inc(rows_turned, 1)

            def first_sweep(step, loads):
                if step.chunk in BY_PE_1 or not step.ran(CHUNKS):
                    turn_chunk(step, loads, 1)
                if step.ran(TURN_LAG):
                    q = step.back(TURN_LAG)
                    if isinstance(step.q0, int) and q.j < CHUNKS:
                        pe.wait_ge(w0_lo, q.j + 1)
                    project(q)
                if step.chunk == 2 and step.ran(CHUNKS):
                    turn_rows(step.back(3))
                if step.ran(SPEC_LAG):
                    spectrum_part(step.back(SPEC_LAG))

            for j in range(PAIR):
                first_sweep(Step(j), 16)
            with pe.Fori(1, PAIRS) as pair:
                q0, b0 = pe.snap(pair * PAIR), pe.snap(pair * 2)
                loads = pe.snap(q0 + 16)
                for j in range(PAIR):
                    first_sweep(Step(j, q0, b0), loads)

            for s in range(STEPS, TAIL_END):
                if s >= SWEEP2:
                    turn_chunk(second(s), None, 2)
                if s < STEPS + TURN_LAG:
                    project(Step(s - TURN_LAG))
                if s >= SWEEP2 + TURN_LAG:
                    q = second(s).back(TURN_LAG)
                    if q.j < STEPS + CHUNKS:
                        pe.wait_ge(sp_lo, q.j - STEPS + 1)
                    project(q)
                if s < STEPS + SPEC_LAG:
                    spectrum_part(Step(s - SPEC_LAG))
                if s == STEPS + 2:
                    turn_rows(Step(s - 3))
                c = s - SP_TURN
                if 0 <= c < CHUNKS:
                    wide = Step(c).wide
                    pe.wait_ge(summed, STEPS - CHUNKS + 2 * wide + 2)
                    if c == 0:
                        pe.wait_ge(x_ready, BLOCKS)
                    else:
                        pe.wait_ge(sp_scaled, c)
                    for k in range(TK):
                        last = nc.tensor.transpose(prod[1][:, k * P:(k + 1) * P],
                                                   ordered(spec[:, wide * WIDE:(wide + 1) * WIDE],
                                                           Step(c).half, k), ident[:])
                    last.then_inc(sp_turned, 1)
                if s >= SWEEP2 and second(s).j == STEPS + CHUNKS + 2:
                    turn_rows(second(s).back(3))
            for j in range(PAIR - TURN_LAG, PAIR):
                project(Step(STEPS + j))
            with pe.Fori(PAIRS + 1, 2 * PAIRS) as pair:
                q0, b0 = pe.snap(pair * PAIR), pe.snap(pair * 2)
                for i in range(2):
                    q = [Step(i * CHUNKS + c, q0, b0) for c in range(CHUNKS)]
                    for c in BY_PE:
                        turn_chunk(q[c], q0, 2)
                    for c in range(CHUNKS):
                        pe.wait_ge(*split(q[c].block(), c))
                        project(q[c], at2[c])
                        if c == 1:
                            turn_rows(q[0].back(1))
            turn_rows(Step(2 * STEPS - 1))


_INS = ['x', 'adj', 'L0_gnn_W', 'L1_gnn_evals', 'L1_gnn_t']
_OUTS = [((4096, 128), 'float32')]


def kernel(**inputs):
    import numpy as _np
    import concourse.bacc as _bacc
    from concourse import mybir as _mybir
    from concourse.bass_utils import run_bass_kernel_spmd as _run

    nc = _bacc.Bacc("TRN2", target_bir_lowering=False, num_devices=1)
    arrays, args = {}, []
    for name in _INS:
        a = _np.ascontiguousarray(inputs[name])
        arrays[f"in_{name}_dram"] = a
        args.append(nc.dram_tensor(f"in_{name}_dram", a.shape, _mybir.dt.from_np(a.dtype), kind="ExternalInput").ap())
    for i, (shape, dtype) in enumerate(_OUTS):
        dt = _mybir.dt.from_np(_np.dtype(dtype))
        args.append(nc.dram_tensor(f"out_{i}_dram", shape, dt, kind="ExternalOutput").ap())
    program(nc, *args)
    r = _run(nc, [arrays], core_ids=[0])
    return r.results[0]["out_0_dram"]
```
